# Optimizing a Trainium2 kernel written in Bass

```python
import numpy as np
import jax
import jax.numpy as jnp

def _softmax(x, axis=-1):
    return jax.nn.softmax(x, axis=axis)

def _gelu(x):
    return jax.nn.gelu(x, approximate=True)

def _silu(x):
    return jax.nn.silu(x)

def _sigmoid(x):
    return jax.nn.sigmoid(x)

def _layernorm(x, axis=-1, eps=1e-05):
    m = jnp.mean(x, axis=axis, keepdims=True)
    v = jnp.var(x, axis=axis, keepdims=True)
    return (x - m) / jnp.sqrt(v + eps)

def _scatter_add(tgt, idx, src, axis=0):
    return tgt.at[idx].add(src)

def _segment_sum(src, seg, n):
    return jax.ops.segment_sum(src, seg, n)
kernel_name = 'mk_adj_resnorm_d4_adj_r2_8dc669'

def setup_inputs(seed: int=0):
    np.random.seed(seed)
    _w = jnp.asarray

    def _rec_inputs():
        import jax
        import jax.numpy as jnp
        _gk = jax.random.key(seed)
        x = -0.0003929 + 0.9999 * jax.random.normal(jax.random.fold_in(_gk, 1), (32, 256, 256), jnp.float32)
        _a = jax.random.bernoulli(jax.random.fold_in(_gk, 2), 0.0625, (32, 256, 256))
        _a = jnp.logical_or(_a, jnp.eye(256, dtype=bool))
        _af = _a.astype(jnp.float32)
        _af = _af * jax.random.uniform(jax.random.fold_in(_gk, 3), (32, 256, 256), jnp.float32, 0.05, 1)
        adj = _af
        _nm = jnp.ones((32, 256), dtype=bool)
        nodemask = _nm
        return (x, adj, nodemask)
    x, adj, nodemask = _rec_inputs()

    def _L0_gnn_setup():
        import jax, jax.numpy as jnp
        import numpy as np
        EPS = 1e-06
        key = jax.random.key(seed)
        k1, k2, k3 = jax.random.split(key, 3)
        B, N, F, O = (8, 2048, 256, 256)
        x = jax.random.normal(k1, (B, N, F), dtype=jnp.float32)
        adj = jax.random.uniform(k2, (B, N, N), dtype=jnp.float32)
        W = jax.random.normal(k3, (O, 2 * F), dtype=jnp.float32) * (1.0 / np.sqrt(2 * F))
        return {'x': x, 'adj': adj, 'W': W}
    _L0_gnn_all = _L0_gnn_setup()
    _L0_gnn_in = {k: v for k, v in _L0_gnn_all.items() if k in ('W',)}
    del _L0_gnn_all

    def _L1_gnn_setup():
        import jax, jax.numpy as jnp
        import numpy as np
        B, N, F_IN, F_HID, F_OUT = (32, 512, 256, 256, 256)

        def _gcn_layer(x, adj, W, b):
            support = jnp.einsum('bnf,fh->bnh', x, W)
            return jnp.einsum('bnm,bmh->bnh', adj, support) + b
        key = jax.random.key(seed)
        ks = jax.random.split(key, 8)

        def xavier(k, fan_in, fan_out):
            bound = float(np.sqrt(6.0 / (fan_in + fan_out)))
            return jax.random.uniform(k, (fan_in, fan_out), jnp.float32, -bound, bound)
        return {'batch_graph': jax.random.normal(ks[0], (B, N, F_IN), jnp.float32), 'adj': jax.random.uniform(ks[1], (B, N, N), jnp.float32), 'W1': xavier(ks[2], F_IN, F_HID), 'b1': jnp.zeros((F_HID,), jnp.float32), 'W2': xavier(ks[3], F_HID, F_HID), 'b2': jnp.zeros((F_HID,), jnp.float32), 'W3': xavier(ks[4], F_HID, F_OUT), 'b3': jnp.zeros((F_OUT,), jnp.float32)}
    _L1_gnn_all = _L1_gnn_setup()
    _L1_gnn_in = {k: v for k, v in _L1_gnn_all.items() if k in ('W1', 'b1', 'W2', 'b2', 'W3', 'b3')}
    del _L1_gnn_all

    def _L2_gnn_setup():
        import jax, jax.numpy as jnp
        import numpy as np
        HEADS = 8
        DIM_HEAD = 64
        LA = 0.33
        LD = 0.33
        LG = 0.33
        key = jax.random.key(seed)
        ks = jax.random.split(key, 6)
        B, N, D = (4, 512, 256)
        inner = HEADS * DIM_HEAD
        x = jax.random.normal(ks[0], (B, N, D), jnp.float32)
        mask = jax.random.uniform(ks[1], (B, N)) < 0.9
        adjacency_mat = (jax.random.uniform(ks[2], (B, N, N)) < 0.05).astype(jnp.float32)
        distance_mat = jax.random.uniform(ks[3], (B, N, N), jnp.float32) * 5.0
        W_qkv = jax.random.normal(ks[4], (D, inner * 3), jnp.float32) * 0.02
        W_out = jax.random.normal(ks[5], (inner, D), jnp.float32) * 0.02
        b_out = jnp.zeros((D,), jnp.float32)
        return {'x': x, 'mask': mask, 'adjacency_mat': adjacency_mat, 'distance_mat': distance_mat, 'W_qkv': W_qkv, 'W_out': W_out, 'b_out': b_out}
    _L2_gnn_all = _L2_gnn_setup()
    _L2_gnn_in = {k: v for k, v in _L2_gnn_all.items() if k in ('W_qkv', 'W_out', 'b_out')}
    del _L2_gnn_all

    def _L3_gnn_setup():
        import jax, jax.numpy as jnp
        import numpy as np
        IN_DIM = 256
        ATT_DIM = 64
        B, N = (4, 2048)
        key = jax.random.key(seed)
        k1, k2, k3, k4 = jax.random.split(key, 4)
        x = jax.random.normal(k1, (B, N, IN_DIM), dtype=jnp.float32)
        adj_matrix = (jax.random.uniform(k2, (B, N, N)) < 0.05).astype(jnp.float32)
        W_qk = jax.random.normal(k3, (2 * ATT_DIM, IN_DIM), dtype=jnp.float32) / np.sqrt(IN_DIM)
        W_v = jax.random.normal(k4, (IN_DIM, IN_DIM), dtype=jnp.float32) / np.sqrt(IN_DIM)
        return {'x': x, 'adj_matrix': adj_matrix, 'W_qk': W_qk, 'W_v': W_v}
    _L3_gnn_all = _L3_gnn_setup()
    _L3_gnn_in = {k: v for k, v in _L3_gnn_all.items() if k in ('W_qk', 'W_v')}
    del _L3_gnn_all
    return {'x': x, 'adj': adj, 'nodemask': nodemask, 'L0_gnn_W': _L0_gnn_in['W'], 'L1_gnn_W1': _L1_gnn_in['W1'], 'L1_gnn_b1': _L1_gnn_in['b1'], 'L1_gnn_W2': _L1_gnn_in['W2'], 'L1_gnn_b2': _L1_gnn_in['b2'], 'L1_gnn_W3': _L1_gnn_in['W3'], 'L1_gnn_b3': _L1_gnn_in['b3'], 'L2_gnn_W_qkv': _L2_gnn_in['W_qkv'], 'L2_gnn_W_out': _L2_gnn_in['W_out'], 'L2_gnn_b_out': _L2_gnn_in['b_out'], 'L3_gnn_W_qk': _L3_gnn_in['W_qk'], 'L3_gnn_W_v': _L3_gnn_in['W_v']}

def reference(x, adj, nodemask, L0_gnn_W, L1_gnn_W1, L1_gnn_b1, L1_gnn_W2, L1_gnn_b2, L1_gnn_W3, L1_gnn_b3, L2_gnn_W_qkv, L2_gnn_W_out, L2_gnn_b_out, L3_gnn_W_qk, L3_gnn_W_v):
    import jax
    import jax.numpy as jnp

    def _L0_gnn_ref(x, adj, W):
        import jax, jax.numpy as jnp
        import numpy as np
        EPS = 1e-06
        deg = jnp.sum(adj, axis=-1, keepdims=True)
        agg = jnp.einsum('bij,bjf->bif', adj, x) / jnp.maximum(deg, EPS)
        cat = jnp.concatenate([x, agg], axis=2)
        out = jnp.einsum('bnf,of->bno', cat, W)
        return jax.nn.relu(out)

    def _L1_gnn_ref(batch_graph, adj, W1, b1, W2, b2, W3, b3):
        import jax, jax.numpy as jnp
        import numpy as np
        B, N, F_IN, F_HID, F_OUT = (32, 512, 256, 256, 256)

        def _gcn_layer(x, adj, W, b):
            support = jnp.einsum('bnf,fh->bnh', x, W)
            return jnp.einsum('bnm,bmh->bnh', adj, support) + b
        x = jax.nn.relu(_gcn_layer(batch_graph, adj, W1, b1))
        x = jax.nn.relu(_gcn_layer(x, adj, W2, b2))
        out = _gcn_layer(x, adj, W3, b3)
        return out

    def _L2_gnn_ref(x, mask, adjacency_mat, distance_mat, W_qkv, W_out, b_out):
        import jax, jax.numpy as jnp
        import numpy as np
        HEADS = 8
        DIM_HEAD = 64
        LA = 0.33
        LD = 0.33
        LG = 0.33
        B, N, _ = x.shape
        scale = DIM_HEAD ** (-0.5)
        qkv = (x @ W_qkv).reshape(B, N, HEADS, 3, DIM_HEAD)
        q, k, v = (jnp.transpose(qkv[..., i, :], (0, 2, 1, 3)) for i in range(3))
        dots = jnp.einsum('bhid,bhjd->bhij', q, k) * scale
        big = jnp.finfo(dots.dtype).max
        m2 = mask[:, None, :, None] & mask[:, None, None, :]
        dots = jnp.where(m2, dots, -big)
        attn = jax.nn.softmax(dots, axis=-1) * LA
        adj = jnp.where(m2, adjacency_mat[:, None], 0.0)
        dist = jnp.where(m2, distance_mat[:, None], big)
        attn = attn + LG * adj + LD * jnp.exp(-dist)
        out = jnp.einsum('bhij,bhjd->bhid', attn, v)
        out = jnp.transpose(out, (0, 2, 1, 3)).reshape(B, N, HEADS * DIM_HEAD)
        return out @ W_out + b_out

    def _L3_gnn_ref(x, adj_matrix, W_qk, W_v):
        import jax, jax.numpy as jnp
        import numpy as np
        IN_DIM = 256
        ATT_DIM = 64
        B, N = (4, 2048)
        qk = jnp.einsum('bnd,ed->bne', x, W_qk)
        q, k = jnp.split(qk, 2, axis=-1)
        v = jnp.einsum('bnd,ed->bne', x, W_v)
        inv_scale = 1.0 / ATT_DIM ** 0.5
        scores = jnp.einsum('bnd,bmd->bnm', q, k) * inv_scale
        w = jnp.sum(scores * adj_matrix, axis=-1, keepdims=True)
        w = jax.nn.softmax(w, axis=1)
        return w * v
    x = _layernorm(x + _L0_gnn_ref(x, adj, L0_gnn_W), axis=-1)
    x = _layernorm(x + _L1_gnn_ref(x, adj, L1_gnn_W1, L1_gnn_b1, L1_gnn_W2, L1_gnn_b2, L1_gnn_W3, L1_gnn_b3), axis=-1)
    x = _layernorm(x + _L2_gnn_ref(x, nodemask, adj, adj, L2_gnn_W_qkv, L2_gnn_W_out, L2_gnn_b_out), axis=-1)
    x = _layernorm(x + _L3_gnn_ref(x, adj, L3_gnn_W_qk, L3_gnn_W_v), axis=-1)
    return x

_drawn_inputs = setup_inputs


def setup_inputs(seed=0):
    import zlib

    import numpy as np

    out = dict(_drawn_inputs(seed))
    spreads = {'L1_gnn_b1': (0.0, 0.1),
     'L1_gnn_b2': (0.0, 0.8),
     'L1_gnn_b3': (0.0, 2.0),
     'L2_gnn_b_out': (0.0, 0.8)}
    factors = {'L3_gnn_W_qk': 8.0, 'L3_gnn_W_v': 8.0}
    for name, (base, spread) in spreads.items():
        noise = np.random.default_rng([zlib.crc32(name.encode()), seed]).standard_normal(out[name].shape)
        drawn = base * np.exp(spread * noise) if base else spread * noise
        out[name] = jnp.asarray(drawn.astype(out[name].dtype))
    for name, factor in factors.items():
        out[name] = (out[name] * factor).astype(out[name].dtype)
    return out
```

```python
from contextlib import ExitStack

import numpy as np
import concourse.bass as bass
from concourse import mybir

F32 = mybir.dt.float32
F32R = mybir.dt.float32r
ALU = mybir.AluOpType
ACT = mybir.ActivationFunctionType
AX = mybir.AxisListType


def graph_blocks_kernel(nc, x, adj, nodemask, L0_W, L1_W1, L1_b1, L1_W2, L1_b2, L1_W3, L1_b3,
                        L2_Wqkv, L2_Wout, L2_bout, L3_Wqk, L3_Wv, out):
    G, N, F = x.shape
    P = 128
    NT = N // P
    FT = F // P
    D = 64
    HEADS = L2_Wout.shape[0] // D
    PAIRS = HEADS // 2
    INNER = HEADS * D
    LN_EPS, DEG_EPS = 1e-5, 1e-6
    MIX = 0.33
    QK_SCALE = D ** -0.5
    BIG = 2.0 ** 100
    L3C = 2 * D + F
    assert (N, F, PAIRS, G % 2) == (256, 256, 4, 0)

    by_node = "g (n p) f -> g p n f"
    x_d, adj_d, out_d = (a.rearrange(by_node, p=P) for a in (x, adj, out))

    ctx = ExitStack()
    with ctx:
        def sb(name, shape, dt=F32):
            return ctx.enter_context(nc.sbuf_tensor(name, shape, dt))

        def sem(name):
            return ctx.enter_context(nc.semaphore(name))

        def sems(name, n=2):
            return [sem(f"{name}_{i}") for i in range(n)]

        w0_raw = sb("w0_raw", [P, F // P, 2 * F])
        w123_raw = sb("w123_raw", [P, 3, FT, F])
        work = sb("work", [P, 2, 2 * NT * 2 * N])
        wqkv_raw = work[:, :, 0:3 * INNER]
        wout_raw = sb("wout_raw", [P, PAIRS, F])
        wqk3_raw = sb("wqk3_raw", [P, F])
        wv3_raw = sb("wv3_raw", [P, FT, F])
        b1_col = sb("b1_col", [P, FT])
        b2_col = sb("b2_col", [P, FT])
        b3_row = sb("b3_row", [P, F])
        bout_row = sb("bout_row", [P, F])
        ident = sb("ident", [P, P])
        one = sb("one", [1, 1])
        minus_half = sb("minus_half", [P, NT])
        w0 = [sb(f"w0_{s}", [P, FT, 2 * F], F32R) for s in "hl"]
        w123 = [sb(f"w123_{s}", [P, 3, FT, F], F32R) for s in "hl"]
        wqkv = [sb(f"wqkv_{s}", [P, FT, 3, INNER], F32R) for s in "hl"]
        wout = [sb(f"wout_{s}", [P, PAIRS, F], F32R) for s in "hl"]
        w3 = [sb(f"w3_{s}", [P, FT, L3C], F32R) for s in "hl"]
        x_sb = sb("x_sb", [P, 2, NT, F])
        adj_sb = sb("adj_sb", [P, 2, NT, N])
        mask_u8 = sb("mask_u8", [1, 2, N], nodemask.dtype)
        mask_row = sb("mask_row", [1, N], F32R)
        mask2 = sb("mask2", [P, NT, N])
        exp_adj = sb("exp_adj", [P, NT, N])
        adj_junk = sb("adj_junk", [P, NT, N])
        deg = sb("deg", [P, NT])
        rdeg = sb("rdeg", [P, NT])
        extra = sb("extra", [P, 2, NT, N])
        minus_big = sb("minus_big", [P, 2, NT, N])
        adjT = [sb(f"adjT_{s}", [P, 2, NT, N], F32R) for s in "hl"]
        fT = [sb(f"fT_{s}", [P, FT, N], F32R) for s in "hl"]
        sup = [sb(f"sup_{s}", [P, NT, F], F32R) for s in "hl"]
        self_part = sb("self_part", [P, NT, F])
        x1_pre = sb("x1_pre", [P, NT, F])
        x1 = sb("x1", [P, NT, F])
        x1_b3 = sb("x1_b3", [P, NT, F])
        hid = sb("hid", [P, FT, N])
        hidT = [sb(f"hidT_{s}", [P, FT, N], F32R) for s in "hl"]
        x2_pre = sb("x2_pre", [P, NT, F])
        x2 = sb("x2", [P, NT, F])
        x2_bout = sb("x2_bout", [P, 2, NT, F])
        x2T = [sb(f"x2T_{s}", [P, FT, N], F32R) for s in "hl"]
        v_sb = sb("v_sb", [P, NT, INNER])
        qT = [sb(f"qT_{s}", [P, 2, N], F32R) for s in "hl"]
        kTz = [sb(f"kTz_{s}", [P, 2, 2, N], F32R) for s in "hl"]
        prob = work[:, 0].rearrange("p (a i h j) -> p a i h j", a=2, i=NT, h=2)
        shift = sb("shift", [P, 2, 2, NT])
        psum_exp = sb("psum_exp", [P, 2, 2, NT])
        rsum = sb("rsum", [P, 2, 2, NT])
        probT = work[:, 1].rearrange("p (a h j i) -> p a h j i", a=2, h=2, j=NT)
        oT = [sb(f"oT_{s}", [P, PAIRS, N], F32R) for s in "hl"]
        x3_pre = sb("x3_pre", [P, NT, F])
        x3 = sb("x3", [P, NT, F])
        x3T = [sb(f"x3T_{s}", [P, FT, N], F32R) for s in "hl"]
        qkv3 = sb("qkv3", [P, NT, L3C])
        k3 = sb("k3", [P, NT, 2, D], F32R)
        gate_junk = sb("gate_junk", [P, NT, 2, D])
        gate = sb("gate", [P, NT])
        gate_max = sb("gate_max", [1, 1])
        gate_shift = sb("gate_shift", [1, 1])
        gate_sum = sb("gate_sum", [1, 1])
        gate_rsum = sb("gate_rsum", [1, 1])
        gate_exp = sb("gate_exp", [1, N])
        gate_prob = sb("gate_prob", [1, N])
        gate_col = sb("gate_col", [P, NT])
        x4_pre = sb("x4_pre", [P, NT, F])
        y_sb = sb("y_sb", [P, 2, NT, F])
        bn = sb("bn", [P, 4, NT, 6])
        mv = sb("mv", [P, 4, NT, 2])
        rstd = sb("rstd", [P, 4, NT])

        bank_f = ctx.enter_context(nc.psum_tensor("bank_f", [P, 3, 512], F32))
        bank_d = ctx.enter_context(nc.psum_tensor("bank_d", [P, 2, 512], F32))
        bank_q = ctx.enter_context(nc.psum_tensor("bank_q", [P, 512], F32))
        bank_t = ctx.enter_context(nc.psum_tensor("bank_t", [P, 512], F32))
        bank_o = ctx.enter_context(nc.psum_tensor("bank_o", [P, 512], F32))

        def halves(ap):
            return ap.rearrange("p (a b) -> p a b", a=2)

        dma_weights, dma_biases = sem("dma_weights"), sem("dma_biases")
        dma_graph = sems("dma_graph")
        dma_out = sem("dma_out")
        pool_const, pool_ident, pool_adj_sum, pool_extra, pool_minus_big = (
            sem(n) for n in ("pool_const", "pool_ident", "pool_adj_sum",
                             "pool_extra", "pool_minus_big"))
        pool_rstd = sems("pool_rstd", 4)
        pool_x1_b3, pool_x2_bout = sem("pool_x1_b3"), sem("pool_x2_bout")
        (pe_w, pe_mask2, pe_xT, pe_adjT, pe_proj0, pe_agg, pe_x1T, pe_gcn, pe_x2T, pe_v, pe_y, pe_x3T,
         pe_proj3, pe_adjk, pe_gate_row, pe_gate_col) = (
            sem(n) for n in ("pe_w", "pe_mask2", "pe_xT", "pe_adjT", "pe_proj0", "pe_agg", "pe_x1T", "pe_gcn",
                             "pe_x2T", "pe_v", "pe_y", "pe_x3T", "pe_proj3", "pe_adjk", "pe_gate_row",
                             "pe_gate_col"))
        pe_sup, pe_hid = sems("pe_sup", 3), sems("pe_hid")
        pe_qk, pe_pv = sems("pe_qk"), sems("pe_pv")
        pe_scores = [sems(f"pe_scores{i}_") for i in range(2)]
        pe_probT = [sems(f"pe_probT{i}_") for i in range(2)]
        (act_w, act_mask_row, act_mask2, act_xT, act_adjT, act_deg, act_exp_adj, act_sup0, act_self, act_x1T, act_x2T, act_v,
         act_x3T, act_qkv3, act_gate_exp, act_gate_col) = (
            sem(n) for n in ("act_w", "act_mask_row", "act_mask2", "act_xT", "act_adjT", "act_deg", "act_exp_adj", "act_sup0", "act_self",
                             "act_x1T", "act_x2T", "act_v", "act_x3T", "act_qkv3", "act_gate_exp",
                             "act_gate_col"))
        act_sup, act_hid = sems("act_sup", 3), sems("act_hid")
        act_qk, act_exp, act_oT = sems("act_qk"), sems("act_exp"), sems("act_oT")
        act_probT = [sems(f"act_probT{i}_") for i in range(2)]
        (dve_w, dve_zero, dve_xT, dve_adjT, dve_deg, dve_rdeg, dve_sup0, dve_agg, dve_x1_pre, dve_x1, dve_x1T,
         dve_x2_pre, dve_x2, dve_x2T, dve_x3_pre, dve_x3, dve_x3T, dve_k3_hi, dve_k3, dve_gate, dve_gate_max,
         dve_gate_shift, dve_gate_rsum, dve_gate_prob, dve_x4_pre, dve_y) = (
            sem(n) for n in ("dve_w", "dve_zero", "dve_xT", "dve_adjT", "dve_deg", "dve_rdeg", "dve_sup0",
                             "dve_agg", "dve_x1_pre", "dve_x1", "dve_x1T", "dve_x2_pre", "dve_x2", "dve_x2T",
                             "dve_x3_pre", "dve_x3", "dve_x3T", "dve_k3_hi", "dve_k3", "dve_gate",
                             "dve_gate_max", "dve_gate_shift", "dve_gate_rsum", "dve_gate_prob", "dve_x4_pre",
                             "dve_y"))
        dve_sup, dve_hid_hi, dve_hid = sems("dve_sup", 3), sems("dve_hid_hi"), sems("dve_hid")
        dve_bn, dve_mv, dve_var = sems("dve_bn", 4), sems("dve_mv", 4), sems("dve_var", 4)
        dve_qk, dve_rsum, dve_oT = sems("dve_qk"), sems("dve_rsum"), sems("dve_oT")
        dve_scores = [sems(f"dve_scores{i}_") for i in range(2)]
        dve_prob = [sems(f"dve_prob{i}_") for i in range(2)]

        def reuse(eng, semaphore, n):
            if not isinstance(n, int) or n > 0:
                eng.wait_ge(semaphore, n)

        class Counts:

            def __init__(self, eng, s):
                keep = (lambda v: v) if isinstance(s, int) else eng.snap
                self.tail = keep(s) if not isinstance(s, int) else s
                self.att = keep(s + 1)
                self.front = keep(s + 2)
                self.two = [keep(2 * s), keep(2 * s + 1), keep(2 * s + 2)]

            def pair(self, p, back=0):
                return self.two[1 + p // 2 - back]

        def slots(eng, slot, last_step=None):
            slot(0, 0, tail=False, front=True)
            with eng.Fori(0, G // 2 - 1) as u:
                slot(2 * u + 1, 1, tail=True, front=True)
                slot(2 * u + 2, 0, tail=True, front=True)
            slot(G - 1, 1, tail=True, front=False)

        WEIGHT_DMAS, BIAS_DMAS = 8, 4
        TILES_W = 5
        block = ctx.enter_context(nc.Block())

        @block.sync
        def _(sp):
            def load(g, b):
                sp.dma_start(x_sb[:, b], x_d[bass.ds(g, 1)].rearrange("g p n f -> (g p) n f")) \
                    .then_inc(dma_graph[b], 16)
                sp.dma_start(adj_sb[:, b], adj_d[bass.ds(g, 1)].rearrange("g p n f -> (g p) n f")) \
                    .then_inc(dma_graph[b], 16)
                sp.dma_start(mask_u8[:, b], nodemask[bass.ds(g, 1)]).then_inc(dma_graph[b], 16)

            def store(g, b):
                sp.dma_start(out_d[bass.ds(g, 1)].rearrange("g p n f -> (g p) n f"), y_sb[:, b]) \
                    .then_inc(dma_out, 16)

            sp.sem_inc(dma_out, 32)
            load(0, 0)
            sp.dma_start(w0_raw[:, :, :], L0_W.rearrange("(n p) f -> p n f", p=P)).then_inc(dma_weights, 16)
            for i, w in enumerate((L1_W1, L1_W2, L1_W3)):
                sp.dma_start(w123_raw[:, i], w.rearrange("(k p) h -> p k h", p=P)).then_inc(dma_weights, 16)
            sp.dma_start(wqkv_raw[:, :, :], L2_Wqkv.rearrange("(k p) h -> p k h", p=P)).then_inc(dma_weights, 16)
            sp.dma_start(wout_raw[:, :, :], L2_Wout.rearrange("(k p) h -> p k h", p=P)).then_inc(dma_weights, 16)
            sp.dma_start(wqk3_raw[:, :], L3_Wqk).then_inc(dma_weights, 16)
            sp.dma_start(wv3_raw[:, :, :], L3_Wv.rearrange("(n p) f -> p n f", p=P)).then_inc(dma_weights, 16)
            sp.dma_start(b1_col[:, :], L1_b1.rearrange("(k p) -> p k", p=P), allow_slow_non_contiguous=True) \
                .then_inc(dma_biases, 16)
            sp.dma_start(b2_col[:, :], L1_b2.rearrange("(k p) -> p k", p=P), allow_slow_non_contiguous=True) \
                .then_inc(dma_biases, 16)
            sp.dma_start(b3_row[:, :], L1_b3.rearrange("(a f) -> a f", a=1).broadcast_to([P, F])) \
                .then_inc(dma_biases, 16)
            sp.dma_start(bout_row[:, :], L2_bout.rearrange("(a f) -> a f", a=1).broadcast_to([P, F])) \
                .then_inc(dma_biases, 16)
            load(1, 1)

            def slot(s, b, tail=True, prefetch=True):
                done = s + 1 if isinstance(s, int) else sp.snap(s + 1)
                if prefetch:
                    g = s + 2 if isinstance(s, int) else sp.snap(s + 2)
                    sp.wait_ge(pool_const, 1)
                    sp.wait_ge(dve_x1_pre, done)
                    sp.wait_ge(pe_adjT, done)
                    sp.wait_ge(pool_adj_sum, done)
                    sp.wait_ge(act_mask_row, done)
                    load(g, b)
                if tail:
                    g = s - 1 if isinstance(s, int) else sp.snap(s - 1)
                    before = 16 * s + 16 if isinstance(s, int) else sp.snap(16 * s + 16)
                    sp.wait_ge(pool_const, 1)
                    sp.wait_ge(dve_y, s if isinstance(s, int) else sp.snap(s + 0))
                    sp.wait_ge(dma_out, before)
                    store(g, 1 - b)

            slot(0, 0, tail=False)
            with sp.Fori(0, G // 2 - 2) as u:
                slot(2 * u + 1, 1)
                slot(2 * u + 2, 0)
            slot(G - 3, 1)
            slot(G - 2, 0, prefetch=False)
            slot(G - 1, 1, prefetch=False)
            slot(G, 0, prefetch=False)
            sp.wait_ge(dma_out, 32 + 16 * G)

        @block.gpsimd
        def _(pool):
            nc.gpsimd.memset(one[:, :], 1.0)
            nc.gpsimd.memset(minus_half[:, :], -0.5).then_inc(pool_const, 1)
            nc.gpsimd.memset(ident[:, :], 0.0).then_inc(pool_ident, 1)
            pool.wait_ge(pool_ident, 1)
            nc.gpsimd.affine_select(out=ident[:, :], in_=ident[:, :], compare_op=ALU.not_equal, fill=1.0,
                                    base=0, pattern=[[-1, P]], channel_multiplier=1).then_inc(pool_ident, 1)

            def front_masks(n, b, before=0):
                pool.wait_ge(act_exp_adj, n)
                nc.gpsimd.tensor_tensor(exp_adj[:, :, :], exp_adj[:, :, :], adj_sb[:, b], ALU.add) \
                    .then_inc(pool_adj_sum, 1)
                pool.wait_ge(pool_adj_sum, n)
                pool.wait_ge(act_mask2, n)
                reuse(pool, dve_x3_pre, before)
                nc.gpsimd.tensor_tensor(extra[:, b], exp_adj[:, :, :], mask2[:, :, :], ALU.mult) \
                    .then_inc(pool_extra, 1)
                nc.gpsimd.tensor_scalar(minus_big[:, b], mask2[:, :, :], 1.0, BIG, ALU.subtract, ALU.mult) \
                    .then_inc(pool_minus_big, 1)

            def norm(k, n):
                pool.wait_ge(dve_var[k], n)
                nc.gpsimd.tensor_tensor(rstd[:, k], mv[:, k, :, 1], minus_half[:, :], ALU.pow) \
                    .then_inc(pool_rstd[k], 1)

            def add_row(src, row, dst, ready, done, n):
                pool.wait_ge(ready, n)
                last = nc.gpsimd.tensor_tensor(dst, src[:, :, :], row[:, :].unsqueeze(1).broadcast_to([P, NT, F]),
                                               ALU.add)
                last.then_inc(done, 1)

            def front(n, b):
                front_masks(n, b)
                norm(0, n)
                add_row(x1, b3_row, x1_b3[:, :, :], dve_x1, pool_x1_b3, n)

            pool.wait_ge(dma_biases, 16 * BIAS_DMAS)
            pool.wait_ge(pool_const, 1)
            front(1, 0)
            norm(1, 1)
            add_row(x2, bout_row, x2_bout[:, 0], dve_x2, pool_x2_bout, 1)

            def slot(s, b, tail, front):
                c = Counts(pool, s)
                if front:
                    front_masks(c.front, 1 - b, c.tail)
                    norm(0, c.front)
                    add_row(x1, b3_row, x1_b3[:, :, :], dve_x1, pool_x1_b3, c.front)
                if tail:
                    norm(3, c.tail)
                norm(2, c.att)
                if front:
                    norm(1, c.front)
                    add_row(x2, bout_row, x2_bout[:, 1 - b], dve_x2, pool_x2_bout, c.front)

            slots(pool, slot)
            norm(3, G)

        @block.scalar
        def _(act):
            def copy(dst, src, scale=1.0):
                return nc.scalar.activation(dst, src, ACT.Copy, scale=scale)

            act.wait_ge(pe_w, 1)
            copy(w0[0][:, :, :], bank_f[:, 0:2, :]).then_inc(act_w, 1)
            act.wait_ge(pe_w, 2)
            copy(w3[0][:, :, :], bank_d[:, :, 0:L3C]).then_inc(act_w, 1)
            act.wait_ge(dma_weights, 16 * WEIGHT_DMAS)
            copy(w123[0][:, :, :, :], w123_raw[:, :, :, :]).then_inc(act_w, 1)
            for k in range(FT):
                last = copy(wqkv[0][:, k].rearrange("p i (h d) -> p i h d", d=D),
                            wqkv_raw[:, k].rearrange("p (h i d) -> p i h d", i=3, d=D))
            last.then_inc(act_w, 1)
            copy(wout[0][:, :, :], wout_raw[:, :, :]).then_inc(act_w, 1)
            act.wait_ge(dma_biases, 16 * BIAS_DMAS)

            def front_mask(n, b, loaded, before=0):
                act.wait_ge(dma_graph[b], loaded)
                reuse(act, pe_mask2, before)
                copy(mask_row[:, :], mask_u8[:, b]).then_inc(act_mask_row, 1)

            def front_x(n, before=0):
                act.wait_ge(pe_mask2, n)
                reuse(act, pool_minus_big, before)
                copy(mask2[:, :, :], halves(bank_f[:, 0])).then_inc(act_mask2, 1)
                act.wait_ge(pe_xT, n)
                copy(fT[0][:, :, :], halves(bank_f[:, 1])).then_inc(act_xT, 1)

            def front_adj_t(n, b, before=0):
                act.wait_ge(pe_adjT, n)
                reuse(act, pe_adjk, before)
                copy(adjT[0][:, b], halves(bank_f[:, 2])).then_inc(act_adjT, 1)

            def front_from_adj(n, b, loaded, before=0):
                act.wait_ge(dma_graph[b], loaded)
                reuse(act, pool_extra, before)
                for t in range(NT):
                    last = nc.scalar.activation(adj_junk[:, t], adj_sb[:, b, t], ACT.Copy, accum_out=deg[:, t:t + 1])
                last.then_inc(act_deg, 1)
                nc.scalar.activation(exp_adj[:, :, :], adj_sb[:, b], ACT.Exp, scale=-1.0).then_inc(act_exp_adj, 1)

            def front_sup0(n):
                act.wait_ge(pe_proj0, n)
                copy(sup[0][:, :, :], bank_f[:, 0:2, F:2 * F]).then_inc(act_sup0, 1)

            def front_self(n):
                act.wait_ge(dve_sup0, n)
                copy(self_part[:, :, :], bank_f[:, 0:2, 0:F]).then_inc(act_self, 1)

            def hi(dst, bank, ready, n, done):
                act.wait_ge(ready, n)
                copy(dst, halves(bank)).then_inc(done, 1)

            def front_hidden(layer, n, bank, bias):
                act.wait_ge(pe_hid[layer], n)
                for h in range(FT):
                    last = nc.scalar.activation(hid[:, h], bank[:, h * N:(h + 1) * N], ACT.Relu,
                                                bias=bias[:, h:h + 1])
                last.then_inc(act_hid[layer], 1)

            def values(n):
                act.wait_ge(pe_v, n)
                copy(v_sb[:, :, :], bank_d[:, :, :], scale=MIX).then_inc(act_v, 1)

            def qk(p, c):
                act.wait_ge(pe_qk[p % 2], c.pair(p))
                copy(qT[0][:, p % 2], bank_q[:, 0:N])
                copy(kTz[0][0:D, p % 2, 0], bank_q[0:D, N:2 * N])
                copy(kTz[0][D:P, p % 2, 1], bank_q[D:P, N:2 * N]).then_inc(act_qk[p % 2], 1)

            def exps(p, c):
                for i in range(NT):
                    act.wait_ge(dve_scores[p % 2][i], c.pair(p))
                    for h in range(2):
                        last = nc.scalar.activation(prob[:, p % 2, i, h], prob[:, p % 2, i, h], ACT.Exp,
                                                    bias=shift[:, p % 2, h, i:i + 1], scale=-1.0,
                                                    accum_out=psum_exp[:, p % 2, h, i:i + 1])
                last.then_inc(act_exp[p % 2], 1)

            def probs_t(p, c):
                for h in range(2):
                    act.wait_ge(pe_probT[p % 2][h], c.pair(p))
                    reuse(act, pe_pv[p % 2], c.pair(p, 1))
                    copy(probT[:, p % 2, h], halves(bank_t[:, :])).then_inc(act_probT[p % 2][h], 1)

            def out_t(p, c):
                act.wait_ge(pe_pv[p % 2], c.pair(p))
                copy(oT[0][:, p], bank_o[:, 0:N]).then_inc(act_oT[p % 2], 1)

            def tail_qkv(n):
                act.wait_ge(pe_proj3, n)
                copy(qkv3[:, :, :], bank_d[:, :, 0:L3C]).then_inc(act_qkv3, 1)

            def tail_exp(n):
                act.wait_ge(dve_gate_shift, n)
                nc.scalar.activation(gate_exp[:, :], bank_o[0:1, 0:N], ACT.Exp, bias=gate_shift[:, :],
                                     accum_out=gate_sum[:, :]).then_inc(act_gate_exp, 1)

            def tail_col(n):
                act.wait_ge(pe_gate_col, n)
                copy(gate_col[:, :], bank_o[:, 0:NT]).then_inc(act_gate_col, 1)

            front_mask(1, 0, 48)
            front_from_adj(1, 0, 48)
            front_x(1)
            front_adj_t(1, 0)
            front_sup0(1)
            front_self(1)
            hi(fT[0][:, :, :], bank_f[:, 0], pe_x1T, 1, act_x1T)
            hi(sup[0][:, :, :], bank_f[:, 1], pe_sup[0], 1, act_sup[0])
            front_hidden(0, 1, bank_f[:, 2], b1_col)
            hi(sup[0][:, :, :], bank_f[:, 0], pe_sup[1], 1, act_sup[1])
            front_hidden(1, 1, bank_f[:, 1], b2_col)
            hi(sup[0][:, :, :], bank_f[:, 2], pe_sup[2], 1, act_sup[2])
            hi(x2T[0][:, :, :], bank_f[:, 1], pe_x2T, 1, act_x2T)

            def slot(s, b, tail, front):
                c = Counts(act, s)
                if front:
                    half = (s + 3) // 2 if isinstance(s, int) else None
                    loaded = 48 * half if half is not None else act.snap(24 * (s + (3 if b else 2)))
                    front_mask(c.front, 1 - b, loaded, c.att)
                values(c.att)
                qk(0, c)
                if tail:
                    hi(x3T[0][:, :, :], bank_o[:, :], pe_x3T, c.tail, act_x3T)
                if front:
                    front_x(c.front, c.att)
                if tail:
                    tail_qkv(c.tail)
                qk(1, c)
                if front:
                    front_from_adj(c.front, 1 - b, loaded, c.att)
                    front_adj_t(c.front, 1 - b, c.tail)
                exps(0, c)
                if front:
                    front_sup0(c.front)
                qk(2, c)
                if tail:
                    tail_exp(c.tail)
                if front:
                    front_self(c.front)
                exps(1, c)
                probs_t(0, c)
                qk(3, c)
                if tail:
                    tail_col(c.tail)
                out_t(0, c)
                exps(2, c)
                probs_t(1, c)
                if front:
                    hi(fT[0][:, :, :], bank_f[:, 0], pe_x1T, c.front, act_x1T)
                out_t(1, c)
                exps(3, c)
                if front:
                    hi(sup[0][:, :, :], bank_f[:, 1], pe_sup[0], c.front, act_sup[0])
                probs_t(2, c)
                if front:
                    front_hidden(0, c.front, bank_f[:, 2], b1_col)
                out_t(2, c)
                if front:
                    hi(sup[0][:, :, :], bank_f[:, 0], pe_sup[1], c.front, act_sup[1])
                probs_t(3, c)
                if front:
                    front_hidden(1, c.front, bank_f[:, 1], b2_col)
                out_t(3, c)
                if front:
                    hi(sup[0][:, :, :], bank_f[:, 2], pe_sup[2], c.front, act_sup[2])
                    act.wait_ge(pe_qk[1], c.pair(3))
                    hi(x2T[0][:, :, :], bank_f[:, 1], pe_x2T, c.front, act_x2T)

            slots(act, slot)
            hi(x3T[0][:, :, :], bank_o[:, :], pe_x3T, G, act_x3T)
            tail_qkv(G)
            tail_exp(G)
            tail_col(G)

        @block.vector
        def _(dve):
            V = nc.vector

            def f32(ap):
                return ap.bitcast(F32)

            def lo(dst, src, hi_part):
                return V.tensor_tensor(dst, src, f32(hi_part), ALU.subtract)

            for part in range(2):
                V.memset(f32(kTz[part][D:P, :, 0]), 0.0)
                V.memset(f32(kTz[part][0:D, :, 1]), 0.0).then_inc(dve_zero, 1)
            dve.wait_ge(act_w, 1)
            lo(w0[1][:, :, :], bank_f[:, 0:2, :], w0[0][:, :, :]).then_inc(dve_w, 1)
            dve.wait_ge(act_w, 2)
            lo(w3[1][:, :, :], bank_d[:, :, 0:L3C], w3[0][:, :, :]).then_inc(dve_w, 1)
            dve.wait_ge(act_w, 3)
            lo(w123[1][:, :, :, :], w123_raw[:, :, :, :], w123[0][:, :, :, :]).then_inc(dve_w, 1)
            dve.wait_ge(act_w, 4)
            for k in range(FT):
                for i in range(3):
                    last = lo(wqkv[1][:, k, i].rearrange("p (h d) -> p h d", d=D),
                              wqkv_raw[:, k].rearrange("p (h i d) -> p i h d", i=3, d=D)[:, i],
                              wqkv[0][:, k, i].rearrange("p (h d) -> p h d", d=D))
            last.then_inc(dve_w, 1)
            dve.wait_ge(act_w, 5)
            lo(wout[1][:, :, :], wout_raw[:, :, :], wout[0][:, :, :]).then_inc(dve_w, 1)

            def split(parts, src, ready, n, done):
                dve.wait_ge(ready, n)
                lo(parts[1], src, parts[0]).then_inc(done, 1)

            def fixed_wait():
                dve.wait_ge(dve_zero, 2)

            def norm_stats(k, src, ready, n):
                dve.wait_ge(ready, n)
                for t in range(NT):
                    last = V.bn_stats(out=bn[:, k, t], in_=src[:, t])
                last.then_inc(dve_bn[k], 1)
                fixed_wait()
                dve.wait_ge(dve_bn[k], n)
                for t in range(NT):
                    last = V.bn_aggr(out=mv[:, k, t], in_=bn[:, k, t])
                last.then_inc(dve_mv[k], 1)
                dve.wait_ge(dve_mv[k], n)
                V.tensor_scalar(mv[:, k, :, 1], mv[:, k, :, 1], LN_EPS, None, ALU.add).then_inc(dve_var[k], 1)

            def norm_apply(k, src, dst, n, done):
                dve.wait_ge(pool_rstd[k], n)
                for t in range(NT):
                    last = V.tensor_scalar(dst[:, t], src[:, t], mv[:, k, t, 0:1], rstd[:, k, t:t + 1],
                                           ALU.subtract, ALU.mult)
                last.then_inc(done, 1)

            def front_x(n):
                split([a[:, :, :] for a in fT], halves(bank_f[:, 1]), act_xT, n, dve_xT)

            def front_adj_t(n, b):
                split([a[:, b] for a in adjT], halves(bank_f[:, 2]), act_adjT, n, dve_adjT)

            def front_degrees(n):
                dve.wait_ge(act_deg, n)
                V.tensor_scalar(rdeg[:, :], deg[:, :], DEG_EPS, None, ALU.max).then_inc(dve_deg, 1)
                dve.wait_ge(dve_deg, n)
                V.reciprocal(rdeg[:, :], rdeg[:, :]).then_inc(dve_rdeg, 1)

            def front_sup0(n):
                split([a[:, :, :] for a in sup], bank_f[:, 0:2, F:2 * F], act_sup0, n, dve_sup0)

            def front_agg(n, b):
                dve.wait_ge(pe_agg, n)
                dve.wait_ge(act_self, n)
                dve.wait_ge(dve_rdeg, n)
                for t in range(NT):
                    last = V.scalar_tensor_tensor(out=x1_pre[:, t], in0=bank_f[:, 2, t * F:(t + 1) * F],
                                                  scalar=rdeg[:, t:t + 1], in1=self_part[:, t],
                                                  op0=ALU.mult, op1=ALU.add)
                last.then_inc(dve_agg, 1)
                dve.wait_ge(dve_agg, n)
                V.scalar_tensor_tensor(out=x1_pre[:, :, :], in0=x1_pre[:, :, :], scalar=0.0, in1=x_sb[:, b],
                                       op0=ALU.max, op1=ALU.add).then_inc(dve_x1_pre, 1)
                norm_stats(0, x1_pre, dve_x1_pre, n)

            def front_hidden(layer, n):
                dve.wait_ge(act_hid[layer], n)
                V.tensor_copy(hidT[0][:, :, :], hid[:, :, :]).then_inc(dve_hid_hi[layer], 1)
                dve.wait_ge(dve_hid_hi[layer], n)
                lo(hidT[1][:, :, :], hid[:, :, :], hidT[0][:, :, :]).then_inc(dve_hid[layer], 1)

            def front_out(n):
                dve.wait_ge(pe_gcn, n)
                dve.wait_ge(pool_x1_b3, n)
                V.tensor_tensor(x2_pre[:, :, :], halves(bank_f[:, 0]), x1_b3[:, :, :], ALU.add) \
                    .then_inc(dve_x2_pre, 1)
                norm_stats(1, x2_pre, dve_x2_pre, n)

            def qk(p, c):
                dve.wait_ge(act_qk[p % 2], c.pair(p))
                lo(qT[1][:, p % 2], bank_q[:, 0:N], qT[0][:, p % 2])
                lo(kTz[1][0:D, p % 2, 0], bank_q[0:D, N:2 * N], kTz[0][0:D, p % 2, 0])
                lo(kTz[1][D:P, p % 2, 1], bank_q[D:P, N:2 * N], kTz[0][D:P, p % 2, 1]).then_inc(dve_qk[p % 2], 1)

            def scores(p, c, b):
                for i in range(NT):
                    fixed_wait()
                    dve.wait_ge(pe_scores[p % 2][i], c.pair(p))
                    for h in range(2):
                        last = V.tensor_tensor_reduce(
                            out=prob[:, p % 2, i, h], in0=bank_d[:, i, h * N:(h + 1) * N],
                            in1=minus_big[:, b, i], scale=-QK_SCALE, scalar=3.0e38, op0=ALU.add, op1=ALU.min,
                            accum_out=shift[:, p % 2, h, i:i + 1])
                    last.then_inc(dve_scores[p % 2][i], 1)

            def probs(p, c, b):
                dve.wait_ge(act_exp[p % 2], c.pair(p))
                V.reciprocal(rsum[:, p % 2], psum_exp[:, p % 2]).then_inc(dve_rsum[p % 2], 1)
                dve.wait_ge(dve_rsum[p % 2], c.pair(p))
                for h in range(2):
                    for i in range(NT):
                        last = V.scalar_tensor_tensor(out=prob[:, p % 2, i, h], in0=prob[:, p % 2, i, h],
                                                      scalar=rsum[:, p % 2, h, i:i + 1], in1=extra[:, b, i],
                                                      op0=ALU.mult, op1=ALU.add)
                    last.then_inc(dve_prob[p % 2][h], 1)

            def out_t(p, c):
                dve.wait_ge(act_oT[p % 2], c.pair(p))
                lo(oT[1][:, p], bank_o[:, 0:N], oT[0][:, p]).then_inc(dve_oT[p % 2], 1)

            def attention_out(n, b):
                dve.wait_ge(pe_y, n)
                dve.wait_ge(pool_x2_bout, n)
                V.tensor_tensor(x3_pre[:, :, :], halves(bank_t[:, :]), x2_bout[:, b], ALU.add) \
                    .then_inc(dve_x3_pre, 1)
                norm_stats(2, x3_pre, dve_x3_pre, n)

            def tail_k(n):
                dve.wait_ge(act_qkv3, n)
                V.tensor_copy(k3[:, :, 0], qkv3[:, :, D:2 * D]).then_inc(dve_k3_hi, 1)
                dve.wait_ge(dve_k3_hi, n)
                lo(k3[:, :, 1], qkv3[:, :, D:2 * D], k3[:, :, 0]).then_inc(dve_k3, 1)

            def tail_gate(n):
                dve.wait_ge(pe_adjk, n)
                for t in range(NT):
                    last = V.tensor_tensor_reduce(
                        out=gate_junk[:, t], in0=bank_o[:, t * P:(t + 1) * P].rearrange("p (a d) -> p a d", a=2),
                        in1=qkv3[:, t, 0:D].unsqueeze(1).broadcast_to([P, 2, D]), scale=QK_SCALE, scalar=0.0,
                        op0=ALU.mult, op1=ALU.add, accum_out=gate[:, t:t + 1])
                last.then_inc(dve_gate, 1)

            def tail_max(n):
                dve.wait_ge(pe_gate_row, n)
                V.tensor_reduce(gate_max[:, :], bank_o[0:1, 0:N], AX.X, ALU.max).then_inc(dve_gate_max, 1)
                dve.wait_ge(dve_gate_max, n)
                V.tensor_scalar(gate_shift[:, :], gate_max[:, :], -1.0, None, ALU.mult).then_inc(dve_gate_shift, 1)

            def tail_prob(n):
                dve.wait_ge(act_gate_exp, n)
                V.reciprocal(gate_rsum[:, :], gate_sum[:, :]).then_inc(dve_gate_rsum, 1)
                dve.wait_ge(dve_gate_rsum, n)
                V.tensor_scalar(gate_prob[:, :], gate_exp[:, :], gate_rsum[:, :], None, ALU.mult) \
                    .then_inc(dve_gate_prob, 1)

            def tail_out(n):
                dve.wait_ge(act_gate_col, n)
                for t in range(NT):
                    last = V.scalar_tensor_tensor(out=x4_pre[:, t], in0=qkv3[:, t, 2 * D:L3C],
                                                  scalar=gate_col[:, t:t + 1], in1=x3[:, t],
                                                  op0=ALU.mult, op1=ALU.add)
                last.then_inc(dve_x4_pre, 1)
                norm_stats(3, x4_pre, dve_x4_pre, n)

            def tail_store(n, b, stored):
                dve.wait_ge(dma_out, stored)
                norm_apply(3, x4_pre, y_sb[:, b], n, dve_y)

            front_x(1)
            front_adj_t(1, 0)
            front_degrees(1)
            front_sup0(1)
            front_agg(1, 0)
            norm_apply(0, x1_pre, x1, 1, dve_x1)
            split([a[:, :, :] for a in fT], halves(bank_f[:, 0]), act_x1T, 1, dve_x1T)
            split([a[:, :, :] for a in sup], halves(bank_f[:, 1]), act_sup[0], 1, dve_sup[0])
            front_hidden(0, 1)
            split([a[:, :, :] for a in sup], halves(bank_f[:, 0]), act_sup[1], 1, dve_sup[1])
            front_hidden(1, 1)
            split([a[:, :, :] for a in sup], halves(bank_f[:, 2]), act_sup[2], 1, dve_sup[2])
            front_out(1)
            norm_apply(1, x2_pre, x2, 1, dve_x2)
            split([a[:, :, :] for a in x2T], halves(bank_f[:, 1]), act_x2T, 1, dve_x2T)

            def slot(s, b, tail, front):
                c = Counts(dve, s)
                dve.wait_ge(pool_minus_big, c.att)
                qk(0, c)
                if tail:
                    split([a[:, :, :] for a in x3T], halves(bank_o[:, :]), act_x3T, c.tail, dve_x3T)
                if front:
                    front_x(c.front)
                if tail:
                    tail_k(c.tail)
                qk(1, c)
                if front:
                    front_degrees(c.front)
                    front_adj_t(c.front, 1 - b)
                scores(0, c, b)
                if tail:
                    tail_gate(c.tail)
                if front:
                    front_sup0(c.front)
                probs(0, c, b)
                qk(2, c)
                if tail:
                    tail_max(c.tail)
                scores(1, c, b)
                if front:
                    front_agg(c.front, 1 - b)
                if tail:
                    tail_prob(c.tail)
                qk(3, c)
                probs(1, c, b)
                if front:
                    norm_apply(0, x1_pre, x1, c.front, dve_x1)
                out_t(0, c)
                scores(2, c, b)
                if tail:
                    tail_out(c.tail)
                if front:
                    split([a[:, :, :] for a in fT], halves(bank_f[:, 0]), act_x1T, c.front, dve_x1T)
                probs(2, c, b)
                out_t(1, c)
                scores(3, c, b)
                if front:
                    split([a[:, :, :] for a in sup], halves(bank_f[:, 1]), act_sup[0], c.front, dve_sup[0])
                if tail:
                    tail_store(c.tail, 1 - b, 16 * s + 0 if isinstance(s, int) else dve.snap(16 * s))
                probs(3, c, b)
                if front:
                    front_hidden(0, c.front)
                out_t(2, c)
                if front:
                    split([a[:, :, :] for a in sup], halves(bank_f[:, 0]), act_sup[1], c.front, dve_sup[1])
                    front_hidden(1, c.front)
                out_t(3, c)
                if front:
                    split([a[:, :, :] for a in sup], halves(bank_f[:, 2]), act_sup[2], c.front, dve_sup[2])
                attention_out(c.att, b)
                if front:
                    front_out(c.front)
                norm_apply(2, x3_pre, x3, c.att, dve_x3)
                if front:
                    norm_apply(1, x2_pre, x2, c.front, dve_x2)
                    split([a[:, :, :] for a in x2T], halves(bank_f[:, 1]), act_x2T, c.front, dve_x2T)

            slots(dve, slot)
            split([a[:, :, :] for a in x3T], halves(bank_o[:, :]), act_x3T, G, dve_x3T)
            tail_k(G)
            tail_gate(G)
            tail_max(G)
            tail_prob(G)
            tail_out(G)
            tail_store(G, 1, 16 * G)

        @block.tensor
        def _(pe):
            mm = nc.tensor.matmul
            PASSES = ((0, 0), (0, 1), (1, 0))

            def product(dst, terms):
                count = len(terms) * len(PASSES)
                n = 0
                for left, right in terms:
                    for a, b in PASSES:
                        last = mm(dst, left[a], right[b], start=n == 0, stop=n == count - 1)
                        n += 1
                return last

            def cut(parts, *index):
                return [a[index] for a in parts]

            A = slice(None)

            def block_of(i, size=P):
                return slice(i * size, (i + 1) * size)

            def transpose_tiles(bank, src):
                for r in range(2):
                    for t in range(2):
                        last = nc.tensor.transpose(bank[:, r * N + t * P:r * N + (t + 1) * P],
                                                   src[:, t, block_of(r)], ident[:, :])
                return last

            pe.wait_ge(pool_ident, 2)
            pe.wait_ge(dma_weights, 16 * WEIGHT_DMAS)
            for k in range(FT):
                for part in range(2):
                    for o in range(FT):
                        last = nc.tensor.transpose(bank_f[:, k, part * F + o * P:part * F + (o + 1) * P],
                                                   w0_raw[:, o, part * F + k * P:part * F + (k + 1) * P],
                                                   ident[:, :])
            last.then_inc(pe_w, 1)
            for k in range(FT):
                nc.tensor.transpose(bank_d[:, k, 0:P], wqk3_raw[:, block_of(k)], ident[:, :])
                for o in range(FT):
                    last = nc.tensor.transpose(bank_d[:, k, P + o * P:P + (o + 1) * P],
                                               wv3_raw[:, o, block_of(k)], ident[:, :])
            last.then_inc(pe_w, 1)
            pe.wait_ge(dve_w, TILES_W)
            pe.wait_ge(dve_zero, 2)

            def front_transposes(n, b, loaded, before=0):
                pe.wait_ge(act_mask_row, n)
                for t in range(NT):
                    last = mm(bank_f[:, 0, t * N:(t + 1) * N], mask_row[:, block_of(t)], mask_row[:, :],
                              start=True, stop=True)
                last.then_inc(pe_mask2, 1)
                pe.wait_ge(dma_graph[b], loaded)
                reuse(pe, dve_x2T, before)
                transpose_tiles(bank_f[:, 1], x_sb[:, b]).then_inc(pe_xT, 1)
                transpose_tiles(bank_f[:, 2], adj_sb[:, b]).then_inc(pe_adjT, 1)

            def front_project(n):
                pe.wait_ge(dve_xT, n)
                pe.wait_ge(act_mask2, n)
                for t in range(NT):
                    last = product(bank_f[:, t, :], [(cut(fT, A, k, block_of(t)), cut(w0, A, k)) for k in range(FT)])
                last.then_inc(pe_proj0, 1)

            def adj_times_support(bank, b):
                for t in range(NT):
                    last = product(bank[:, t * F:(t + 1) * F],
                                   [(cut(adjT, A, b, k, block_of(t)), cut(sup, A, k)) for k in range(NT)])
                return last

            def front_aggregate(n, b):
                pe.wait_ge(dve_sup0, n)
                pe.wait_ge(dve_adjT, n)
                adj_times_support(bank_f[:, 2], b).then_inc(pe_agg, 1)

            def front_x1_transpose(n):
                pe.wait_ge(dve_x1, n)
                transpose_tiles(bank_f[:, 0], x1).then_inc(pe_x1T, 1)

            def front_support(layer, n, bank, src, ready):
                pe.wait_ge(ready, n)
                for t in range(NT):
                    last = product(bank[:, t * F:(t + 1) * F],
                                   [(cut(src, A, k, block_of(t)), cut(w123, A, layer, k)) for k in range(FT)])
                last.then_inc(pe_sup[layer], 1)

            def front_hidden(layer, n, bank, b):
                pe.wait_ge(dve_sup[layer], n)
                for h in range(FT):
                    last = product(bank[:, h * N:(h + 1) * N],
                                   [(cut(sup, A, k, block_of(h)), cut(adjT, A, b, k)) for k in range(NT)])
                last.then_inc(pe_hid[layer], 1)

            def front_out(n, b):
                pe.wait_ge(dve_sup[2], n)
                adj_times_support(bank_f[:, 0], b).then_inc(pe_gcn, 1)

            def front_x2_transpose(n):
                pe.wait_ge(dve_x2, n)
                transpose_tiles(bank_f[:, 1], x2).then_inc(pe_x2T, 1)

            def values(n):
                pe.wait_ge(dve_x2T, n)
                for t in range(NT):
                    last = product(bank_d[:, t, :],
                                   [(cut(x2T, A, k, block_of(t)), cut(wqkv, A, k, 2)) for k in range(FT)])
                last.then_inc(pe_v, 1)

            def qk(p, c):
                reuse(pe, dve_qk[(p - 1) % 2], c.pair(p - 1) if p else c.two[0])
                for i in range(2):
                    last = product(bank_q[:, i * N:(i + 1) * N],
                                   [(cut(wqkv, A, k, i, block_of(p)), cut(x2T, A, k)) for k in range(FT)])
                last.then_inc(pe_qk[p % 2], 1)

            def scores(p, c):
                pe.wait_ge(dve_qk[p % 2], c.pair(p))
                for i in range(NT):
                    if p:
                        pe.wait_ge(dve_scores[(p - 1) % 2][i], c.pair(p - 1))
                    product(bank_d[:, i, :],
                            [(cut(qT, A, p % 2, block_of(i)),
                              [a[:, p % 2].rearrange("p h n -> p (h n)") for a in kTz])]) \
                        .then_inc(pe_scores[p % 2][i], 1)

            def probs_t(p, c, before):
                for h in range(2):
                    pe.wait_ge(dve_prob[p % 2][h], c.pair(p))
                    if h:
                        pe.wait_ge(act_probT[p % 2][0], c.pair(p))
                    elif p:
                        pe.wait_ge(act_probT[(p - 1) % 2][1], c.pair(p - 1))
                    else:
                        reuse(pe, dve_x3_pre, before)
                    transpose_tiles(bank_t[:, :], prob[:, p % 2, :, h]).then_inc(pe_probT[p % 2][h], 1)

            def attend(p, c, bank_free, free_at):
                pe.wait_ge(act_probT[p % 2][1], c.pair(p))
                if p == 0:
                    pe.wait_ge(act_v, c.att)
                reuse(pe, bank_free, free_at)
                for k in range(NT):
                    for h in range(2):
                        last = mm(bank_o[h * D:(h + 1) * D, 0:N], v_sb[:, k, (2 * p + h) * D:(2 * p + h + 1) * D],
                                  probT[:, p % 2, h, k], start=k == 0, stop=k == NT - 1)
                last.then_inc(pe_pv[p % 2], 1)

            def project_out(c):
                pe.wait_ge(dve_oT[0], c.pair(2))
                pe.wait_ge(dve_oT[1], c.pair(3))
                for t in range(NT):
                    last = product(bank_t[:, t * F:(t + 1) * F],
                                   [(cut(oT, A, p, block_of(t)), cut(wout, A, p)) for p in range(PAIRS)])
                last.then_inc(pe_y, 1)

            def tail_transpose(n):
                pe.wait_ge(dve_x3, n)
                transpose_tiles(bank_o[:, :], x3).then_inc(pe_x3T, 1)

            def tail_project(n, after_v):
                pe.wait_ge(dve_x3T, n)
                reuse(pe, act_v, after_v)
                for t in range(NT):
                    last = product(bank_d[:, t, 0:L3C],
                                   [(cut(x3T, A, k, block_of(t)), cut(w3, A, k)) for k in range(FT)])
                last.then_inc(pe_proj3, 1)

            def tail_adj_k(n, b):
                pe.wait_ge(dve_k3, n)
                for t in range(NT):
                    at = t * P
                    for k in range(NT):
                        mm(bank_o[:, at:at + 2 * D], adjT[0][:, b, k, block_of(t)],
                           k3[:, k].rearrange("p a d -> p (a d)"), start=k == 0, stop=False)
                    for k in range(NT):
                        last = mm(bank_o[:, at:at + D], adjT[1][:, b, k, block_of(t)], k3[:, k, 0],
                                  start=False, stop=k == NT - 1)
                last.then_inc(pe_adjk, 1)

            def tail_gate_row(n):
                pe.wait_ge(dve_gate, n)
                for t in range(NT):
                    last = nc.tensor.transpose(bank_o[0:1, t * P:(t + 1) * P], gate[:, t:t + 1], ident[:, :])
                last.then_inc(pe_gate_row, 1)

            def tail_gate_col(n):
                pe.wait_ge(dve_gate_prob, n)
                for t in range(NT):
                    last = mm(bank_o[:, t:t + 1], gate_prob[:, block_of(t)], one[:, :], start=True, stop=True)
                last.then_inc(pe_gate_col, 1)

            front_transposes(1, 0, 48)
            front_project(1)
            front_aggregate(1, 0)
            front_x1_transpose(1)
            front_support(0, 1, bank_f[:, 1], fT, dve_x1T)
            front_hidden(0, 1, bank_f[:, 2], 0)
            front_support(1, 1, bank_f[:, 0], hidT, dve_hid[0])
            front_hidden(1, 1, bank_f[:, 1], 0)
            front_support(2, 1, bank_f[:, 2], hidT, dve_hid[1])
            front_out(1, 0)
            front_x2_transpose(1)

            def slot(s, b, tail, front):
                c = Counts(pe, s)
                values(c.att)
                qk(0, c)
                if tail:
                    tail_transpose(c.tail)
                if front:
                    half = (s + 3) // 2 if isinstance(s, int) else None
                    loaded = 48 * half if half is not None else pe.snap(24 * (s + (3 if b else 2)))
                    front_transposes(c.front, 1 - b, loaded, c.att)
                if tail:
                    tail_project(c.tail, c.att)
                qk(1, c)
                if tail:
                    tail_adj_k(c.tail, 1 - b)
                if tail:
                    pe.wait_ge(act_qkv3, c.tail)
                scores(0, c)
                if front:
                    front_project(c.front)
                qk(2, c)
                if tail:
                    tail_gate_row(c.tail)
                scores(1, c)
                probs_t(0, c, c.tail)
                if front:
                    front_aggregate(c.front, 1 - b)
                qk(3, c)
                if tail:
                    tail_gate_col(c.tail)
                    attend(0, c, act_gate_col, c.tail)
                else:
                    attend(0, c, act_v, 0)
                scores(2, c)
                probs_t(1, c, 0)
                if front:
                    front_x1_transpose(c.front)
                attend(1, c, dve_oT[0], c.pair(0))
                scores(3, c)
                if front:
                    front_support(0, c.front, bank_f[:, 1], fT, dve_x1T)
                probs_t(2, c, 0)
                if front:
                    front_hidden(0, c.front, bank_f[:, 2], 1 - b)
                attend(2, c, dve_oT[1], c.pair(1))
                if front:
                    front_support(1, c.front, bank_f[:, 0], hidT, dve_hid[0])
                probs_t(3, c, 0)
                if front:
                    front_hidden(1, c.front, bank_f[:, 1], 1 - b)
                attend(3, c, dve_oT[0], c.pair(2))
                if front:
                    front_support(2, c.front, bank_f[:, 2], hidT, dve_hid[1])
                project_out(c)
                if front:
                    front_out(c.front, 1 - b)
                    front_x2_transpose(c.front)

            slots(pe, slot)
            tail_transpose(G)
            tail_project(G, 0)
            tail_adj_k(G, 1)
            tail_gate_row(G)
            tail_gate_col(G)


_INS = ["x", "adj", "nodemask", "L0_gnn_W", "L1_gnn_W1", "L1_gnn_b1", "L1_gnn_W2", "L1_gnn_b2", "L1_gnn_W3",
        "L1_gnn_b3", "L2_gnn_W_qkv", "L2_gnn_W_out", "L2_gnn_b_out", "L3_gnn_W_qk", "L3_gnn_W_v"]


def kernel(**inputs):
    import numpy as _np
    import concourse.bacc as _bacc
    from concourse import mybir as _mybir
    from concourse.bass_utils import run_bass_kernel_spmd as _run

    nc = _bacc.Bacc("TRN2", target_bir_lowering=False, num_devices=1)
    arrays, args = {}, []
    for name in _INS:
        a = _np.ascontiguousarray(inputs[name])
        arrays[f"in_{name}"] = a
        args.append(nc.dram_tensor(f"in_{name}", a.shape, _mybir.dt.from_np(a.dtype), kind="ExternalInput").ap())
    args.append(nc.dram_tensor("out_0", inputs["x"].shape, F32, kind="ExternalOutput").ap())
    graph_blocks_kernel(nc, *args)
    r = _run(nc, [arrays], core_ids=[0])
    return r.results[0]["out_0"]
```

```python
from contextlib import ExitStack

import numpy as np
import concourse.bass as bass
from concourse import mybir

F32 = mybir.dt.float32
F32R = mybir.dt.float32r
ALU = mybir.AluOpType
ACT = mybir.ActivationFunctionType
AX = mybir.AxisListType


def graph_blocks_kernel(nc, x, adj, nodemask, L0_W, L1_W1, L1_b1, L1_W2, L1_b2, L1_W3, L1_b3,
                        L2_Wqkv, L2_Wout, L2_bout, L3_Wqk, L3_Wv, out):
    G, N, F = x.shape
    P = 128
    NT = N // P
    FT = F // P
    D = 64
    HEADS = L2_Wout.shape[0] // D
    PAIRS = HEADS // 2
    INNER = HEADS * D
    LN_EPS, DEG_EPS = 1e-5, 1e-6
    MIX = 0.33
    QK_SCALE = D ** -0.5
    BIG = 2.0 ** 100
    L3C = 2 * D + F
    assert (N, F, PAIRS, G % 2) == (256, 256, 4, 0)

    by_node = "g (n p) f -> g p n f"
    x_d, adj_d, out_d = (a.rearrange(by_node, p=P) for a in (x, adj, out))

    ctx = ExitStack()
    with ctx:
        def sb(name, shape, dt=F32):
            return ctx.enter_context(nc.sbuf_tensor(name, shape, dt))

        def sem(name):
            return ctx.enter_context(nc.semaphore(name))

        def sems(name, n=2):
            return [sem(f"{name}_{i}") for i in range(n)]

        w0_raw = sb("w0_raw", [P, F // P, 2 * F])
        w123_raw = sb("w123_raw", [P, 3, FT, F])
        work = sb("work", [P, 2, 2 * NT * 2 * N])
        wqkv_raw = work[:, :, 0:3 * INNER]
        wout_raw = sb("wout_raw", [P, PAIRS, F])
        wqk3_raw = sb("wqk3_raw", [P, F])
        wv3_raw = sb("wv3_raw", [P, FT, F])
        b1_col = sb("b1_col", [P, FT])
        b2_col = sb("b2_col", [P, FT])
        b3_row = sb("b3_row", [P, F])
        bout_row = sb("bout_row", [P, F])
        ident = sb("ident", [P, P])
        one = sb("one", [1, 1])
        minus_half = sb("minus_half", [P, NT])
        eps = sb("eps", [P, NT])
        w0 = [sb(f"w0_{s}", [P, FT, 2 * F], F32R) for s in "hl"]
        w123 = [sb(f"w123_{s}", [P, 3, FT, F], F32R) for s in "hl"]
        wqkv = [sb(f"wqkv_{s}", [P, FT, 3, INNER], F32R) for s in "hl"]
        wout = [sb(f"wout_{s}", [P, PAIRS, F], F32R) for s in "hl"]
        w3 = [sb(f"w3_{s}", [P, FT, L3C], F32R) for s in "hl"]
        x_sb = sb("x_sb", [P, 2, NT, F])
        adj_sb = sb("adj_sb", [P, 2, NT, N])
        mask_u8 = sb("mask_u8", [1, 2, N], nodemask.dtype)
        mask_row = sb("mask_row", [1, N], F32R)
        mask2 = sb("mask2", [P, NT, N])
        exp_adj = sb("exp_adj", [P, NT, N])
        adj_junk = sb("adj_junk", [P, NT, N])
        deg = sb("deg", [P, NT])
        rdeg = sb("rdeg", [P, NT])
        extra = sb("extra", [P, 2, NT, N])
        minus_big = sb("minus_big", [P, 2, NT, N])
        adjT = [sb(f"adjT_{s}", [P, 2, NT, N], F32R) for s in "hl"]
        fT = [sb(f"fT_{s}", [P, FT, N], F32R) for s in "hl"]
        sup = [sb(f"sup_{s}", [P, NT, F], F32R) for s in "hl"]
        self_part = sb("self_part", [P, NT, F])
        x1_pre = sb("x1_pre", [P, NT, F])
        x1 = sb("x1", [P, NT, F])
        x1_b3 = sb("x1_b3", [P, NT, F])
        hid = sb("hid", [P, FT, N])
        hidT = [sb(f"hidT_{s}", [P, FT, N], F32R) for s in "hl"]
        x2_pre = sb("x2_pre", [P, NT, F])
        x2 = sb("x2", [P, NT, F])
        x2_bout = sb("x2_bout", [P, 2, NT, F])
        x2T = [sb(f"x2T_{s}", [P, FT, N], F32R) for s in "hl"]
        v_sb = sb("v_sb", [P, NT, INNER])
        qT = [sb(f"qT_{s}", [P, 2, N], F32R) for s in "hl"]
        kTz = [sb(f"kTz_{s}", [P, 2, 2, N], F32R) for s in "hl"]
        prob = work[:, 0].rearrange("p (a i h j) -> p a i h j", a=2, i=NT, h=2)
        shift = sb("shift", [P, 2, 2, NT])
        psum_exp = sb("psum_exp", [P, 2, 2, NT])
        rsum = sb("rsum", [P, 2, 2, NT])
        probT = work[:, 1].rearrange("p (a h j i) -> p a h j i", a=2, h=2, j=NT)
        oT = [sb(f"oT_{s}", [P, PAIRS, N], F32R) for s in "hl"]
        x3_pre = sb("x3_pre", [P, NT, F])
        x3 = sb("x3", [P, NT, F])
        x3T = [sb(f"x3T_{s}", [P, FT, N], F32R) for s in "hl"]
        qkv3 = sb("qkv3", [P, NT, L3C])
        k3 = sb("k3", [P, NT, 2, D], F32R)
        gate_junk = sb("gate_junk", [P, NT, 2, D])
        gate = sb("gate", [P, NT])
        gate_max = sb("gate_max", [1, 1])
        gate_shift = sb("gate_shift", [1, 1])
        gate_sum = sb("gate_sum", [1, 1])
        gate_rsum = sb("gate_rsum", [1, 1])
        gate_exp = sb("gate_exp", [1, N])
        gate_prob = sb("gate_prob", [1, N])
        gate_col = sb("gate_col", [P, NT])
        x4_pre = sb("x4_pre", [P, NT, F])
        y_sb = sb("y_sb", [P, 2, NT, F])
        bn = sb("bn", [P, 4, NT, 6])
        mv = sb("mv", [P, 4, NT, 2])
        rstd = sb("rstd", [P, 4, NT])

        bank_f = ctx.enter_context(nc.psum_tensor("bank_f", [P, 3, 512], F32))
        bank_d = ctx.enter_context(nc.psum_tensor("bank_d", [P, 2, 512], F32))
        bank_q = ctx.enter_context(nc.psum_tensor("bank_q", [P, 512], F32))
        bank_t = ctx.enter_context(nc.psum_tensor("bank_t", [P, 512], F32))
        bank_o = ctx.enter_context(nc.psum_tensor("bank_o", [P, 512], F32))

        def halves(ap):
            return ap.rearrange("p (a b) -> p a b", a=2)

        dma_weights, dma_biases = sem("dma_weights"), sem("dma_biases")
        dma_graph = sems("dma_graph")
        dma_out = sem("dma_out")
        pool_const, pool_ident, pool_adj_sum, pool_extra, act_minus_big = (
            sem(n) for n in ("pool_const", "pool_ident", "pool_adj_sum",
                             "pool_extra", "act_minus_big"))
        pool_rstd = sems("pool_rstd", 4)
        pool_var, dve_x = sems("pool_var", 4), sems("dve_x", 3)
        pool_centred, pool_y = sem("pool_centred"), sem("pool_y")
        pool_x1_b3, pool_x2_bout, pool_gate_v, pool_x4_pre = (
            sem(n) for n in ("pool_x1_b3", "pool_x2_bout", "pool_gate_v", "pool_x4_pre"))
        (pe_w, pe_mask2, pe_xT, pe_adjT, pe_proj0, pe_agg, pe_x1T, pe_gcn, pe_x2T, pe_v, pe_y, pe_x3T,
         pe_proj3, pe_adjk, pe_gate_row, pe_gate_col) = (
            sem(n) for n in ("pe_w", "pe_mask2", "pe_xT", "pe_adjT", "pe_proj0", "pe_agg", "pe_x1T", "pe_gcn",
                             "pe_x2T", "pe_v", "pe_y", "pe_x3T", "pe_proj3", "pe_adjk", "pe_gate_row",
                             "pe_gate_col"))
        pe_sup, pe_hid = sems("pe_sup", 3), sems("pe_hid")
        pe_qk, pe_pv = sems("pe_qk"), sems("pe_pv")
        pe_scores = [sems(f"pe_scores{i}_") for i in range(2)]
        pe_probT = [sems(f"pe_probT{i}_") for i in range(2)]
        (act_w, act_mask_row, act_mask2, act_xT, act_adjT, act_deg, act_exp_adj, act_sup0, act_self, act_x1T, act_x2T, act_v,
         act_x3T, act_qkv3, act_gate_exp, act_gate_col) = (
            sem(n) for n in ("act_w", "act_mask_row", "act_mask2", "act_xT", "act_adjT", "act_deg", "act_exp_adj", "act_sup0", "act_self",
                             "act_x1T", "act_x2T", "act_v", "act_x3T", "act_qkv3", "act_gate_exp",
                             "act_gate_col"))
        act_sup, act_hid, act_hid_hi = sems("act_sup", 3), sems("act_hid"), sems("act_hid_hi")
        act_qk, act_oT = sems("act_qk"), sems("act_oT")
        act_exp = [sems(f"act_exp{i}_") for i in range(2)]
        act_probT = [sems(f"act_probT{i}_") for i in range(2)]
        (dve_w, dve_zero, dve_xT, dve_adjT, dve_deg, dve_rdeg, dve_sup0, dve_agg, dve_x1_pre, dve_x1T,
         dve_x2_pre, dve_x2T, dve_x3_pre, dve_x3T, dve_k3_hi, dve_k3, dve_gate, dve_gate_max,
         dve_gate_shift, dve_gate_rsum, dve_gate_prob) = (
            sem(n) for n in ("dve_w", "dve_zero", "dve_xT", "dve_adjT", "dve_deg", "dve_rdeg", "dve_sup0",
                             "dve_agg", "dve_x1_pre", "dve_x1T", "dve_x2_pre", "dve_x2T", "dve_x3_pre",
                             "dve_x3T", "dve_k3_hi", "dve_k3", "dve_gate", "dve_gate_max", "dve_gate_shift",
                             "dve_gate_rsum", "dve_gate_prob"))
        dve_sup, dve_hid = sems("dve_sup", 3), sems("dve_hid")
        dve_bn, dve_mv = sems("dve_bn", 4), sems("dve_mv", 4)
        dve_qk, dve_rsum, dve_oT = sems("dve_qk"), sems("dve_rsum"), sems("dve_oT")
        dve_scores = [sems(f"dve_scores{i}_") for i in range(2)]
        dve_prob = [sems(f"dve_prob{i}_") for i in range(2)]

        def reuse(eng, semaphore, n):
            if not isinstance(n, int) or n > 0:
                eng.wait_ge(semaphore, n)

        class Counts:

            def __init__(self, eng, s):
                keep = (lambda v: v) if isinstance(s, int) else eng.snap
                self.tail = keep(s) if not isinstance(s, int) else s
                self.att = keep(s + 1)
                self.front = keep(s + 2)
                self.two = [keep(2 * s), keep(2 * s + 1), keep(2 * s + 2)]

            def pair(self, p, back=0):
                return self.two[1 + p // 2 - back]

        def slots(eng, slot, last_step=None):
            slot(0, 0, tail=False, front=True)
            with eng.Fori(0, G // 2 - 1) as u:
                slot(2 * u + 1, 1, tail=True, front=True)
                slot(2 * u + 2, 0, tail=True, front=True)
            slot(G - 1, 1, tail=True, front=False)

        WEIGHT_DMAS, BIAS_DMAS = 8, 4
        TILES_W = 5
        block = ctx.enter_context(nc.Block())

        @block.sync
        def _(sp):
            def load(g, b):
                sp.dma_start(x_sb[:, b], x_d[bass.ds(g, 1)].rearrange("g p n f -> (g p) n f")) \
                    .then_inc(dma_graph[b], 16)
                sp.dma_start(adj_sb[:, b], adj_d[bass.ds(g, 1)].rearrange("g p n f -> (g p) n f")) \
                    .then_inc(dma_graph[b], 16)
                sp.dma_start(mask_u8[:, b], nodemask[bass.ds(g, 1)]).then_inc(dma_graph[b], 16)

            def store(g, b):
                sp.dma_start(out_d[bass.ds(g, 1)].rearrange("g p n f -> (g p) n f"), y_sb[:, b]) \
                    .then_inc(dma_out, 16)

            sp.sem_inc(dma_out, 32)
            load(0, 0)
            sp.dma_start(w0_raw[:, :, :], L0_W.rearrange("(n p) f -> p n f", p=P)).then_inc(dma_weights, 16)
            for i, w in enumerate((L1_W1, L1_W2, L1_W3)):
                sp.dma_start(w123_raw[:, i], w.rearrange("(k p) h -> p k h", p=P)).then_inc(dma_weights, 16)
            sp.dma_start(wqkv_raw[:, :, :], L2_Wqkv.rearrange("(k p) h -> p k h", p=P)).then_inc(dma_weights, 16)
            sp.dma_start(wout_raw[:, :, :], L2_Wout.rearrange("(k p) h -> p k h", p=P)).then_inc(dma_weights, 16)
            sp.dma_start(wqk3_raw[:, :], L3_Wqk).then_inc(dma_weights, 16)
            sp.dma_start(wv3_raw[:, :, :], L3_Wv.rearrange("(n p) f -> p n f", p=P)).then_inc(dma_weights, 16)
            sp.dma_start(b1_col[:, :], L1_b1.rearrange("(k p) -> p k", p=P), allow_slow_non_contiguous=True) \
                .then_inc(dma_biases, 16)
            sp.dma_start(b2_col[:, :], L1_b2.rearrange("(k p) -> p k", p=P), allow_slow_non_contiguous=True) \
                .then_inc(dma_biases, 16)
            sp.dma_start(b3_row[:, :], L1_b3.rearrange("(a f) -> a f", a=1).broadcast_to([P, F])) \
                .then_inc(dma_biases, 16)
            sp.dma_start(bout_row[:, :], L2_bout.rearrange("(a f) -> a f", a=1).broadcast_to([P, F])) \
                .then_inc(dma_biases, 16)
            load(1, 1)

            def slot(s, b, tail=True, prefetch=True):
                done = s + 1 if isinstance(s, int) else sp.snap(s + 1)
                if prefetch:
                    g = s + 2 if isinstance(s, int) else sp.snap(s + 2)
                    sp.wait_ge(pool_const, 1)
                    sp.wait_ge(dve_x1_pre, done)
                    sp.wait_ge(pe_adjT, done)
                    sp.wait_ge(pool_adj_sum, done)
                    sp.wait_ge(act_mask_row, done)
                    load(g, b)
                if tail:
                    g = s - 1 if isinstance(s, int) else sp.snap(s - 1)
                    before = 16 * s + 16 if isinstance(s, int) else sp.snap(16 * s + 16)
                    sp.wait_ge(pool_const, 1)
                    sp.wait_ge(pool_y, s if isinstance(s, int) else sp.snap(s + 0))
                    sp.wait_ge(dma_out, before)
                    store(g, 1 - b)

            slot(0, 0, tail=False)
            with sp.Fori(0, G // 2 - 2) as u:
                slot(2 * u + 1, 1)
                slot(2 * u + 2, 0)
            slot(G - 3, 1)
            slot(G - 2, 0, prefetch=False)
            slot(G - 1, 1, prefetch=False)
            slot(G, 0, prefetch=False)
            sp.wait_ge(dma_out, 32 + 16 * G)

        @block.gpsimd
        def _(pool):
            nc.gpsimd.memset(one[:, :], 1.0)
            nc.gpsimd.memset(eps[:, :], LN_EPS)
            nc.gpsimd.memset(minus_half[:, :], -0.5).then_inc(pool_const, 1)
            nc.gpsimd.memset(ident[:, :], 0.0).then_inc(pool_ident, 1)
            pool.wait_ge(pool_ident, 1)
            nc.gpsimd.affine_select(out=ident[:, :], in_=ident[:, :], compare_op=ALU.not_equal, fill=1.0,
                                    base=0, pattern=[[-1, P]], channel_multiplier=1).then_inc(pool_ident, 1)

            def front_adj_sum(n, b):
                pool.wait_ge(act_exp_adj, n)
                nc.gpsimd.tensor_tensor(exp_adj[:, :, :], exp_adj[:, :, :], adj_sb[:, b], ALU.add) \
                    .then_inc(pool_adj_sum, 1)

            def front_extra(n, b, prob_before=0):
                pool.wait_ge(pool_adj_sum, n)
                pool.wait_ge(act_mask2, n)
                reuse(pool, dve_prob[1][0], prob_before)
                reuse(pool, dve_prob[1][1], prob_before)
                nc.gpsimd.tensor_tensor(extra[:, b], exp_adj[:, :, :], mask2[:, :, :], ALU.mult) \
                    .then_inc(pool_extra, 1)

            def norm_rstd(k, n):
                pool.wait_ge(dve_mv[k], n)
                nc.gpsimd.tensor_tensor(mv[:, k, :, 1], mv[:, k, :, 1], eps[:, :], ALU.add) \
                    .then_inc(pool_var[k], 1)
                pool.wait_ge(pool_var[k], n)
                nc.gpsimd.tensor_tensor(rstd[:, k], mv[:, k, :, 1], minus_half[:, :], ALU.pow) \
                    .then_inc(pool_rstd[k], 1)

            def columns(ap):
                return ap.unsqueeze(2).broadcast_to([P, NT, F])

            def x1_b3_sum(n, before=0):
                pool.wait_ge(dve_x[0], n)
                reuse(pool, dve_x2_pre, before)
                nc.gpsimd.tensor_tensor(x1_b3[:, :, :], x1[:, :, :],
                                        b3_row[:, :].unsqueeze(1).broadcast_to([P, NT, F]), ALU.add) \
                    .then_inc(pool_x1_b3, 1)

            def x2_bout_sum(n, b):
                pool.wait_ge(dve_x[1], n)
                nc.gpsimd.tensor_tensor(x2_bout[:, b], x2[:, :, :],
                                        bout_row[:, :].unsqueeze(1).broadcast_to([P, NT, F]), ALU.add) \
                    .then_inc(pool_x2_bout, 1)

            def tail_out(n):
                pool.wait_ge(act_gate_col, n)
                nc.gpsimd.tensor_tensor(x4_pre[:, :, :], qkv3[:, :, 2 * D:L3C], columns(gate_col[:, :]), ALU.mult) \
                    .then_inc(pool_gate_v, 1)
                pool.wait_ge(pool_gate_v, n)
                nc.gpsimd.tensor_tensor(x4_pre[:, :, :], x4_pre[:, :, :], x3[:, :, :], ALU.add) \
                    .then_inc(pool_x4_pre, 1)

            def tail_norm(n, b, stored):
                norm_rstd(3, n)
                pool.wait_ge(dma_out, stored)
                nc.gpsimd.tensor_tensor(y_sb[:, b], x4_pre[:, :, :], columns(mv[:, 3, :, 0]), ALU.subtract) \
                    .then_inc(pool_centred, 1)
                pool.wait_ge(pool_centred, n)
                pool.wait_ge(pool_rstd[3], n)
                nc.gpsimd.tensor_tensor(y_sb[:, b], y_sb[:, b], columns(rstd[:, 3]), ALU.mult) \
                    .then_inc(pool_y, 1)

            pool.wait_ge(dma_biases, 16 * BIAS_DMAS)
            pool.wait_ge(pool_const, 1)
            front_adj_sum(1, 0)
            front_extra(1, 0)
            norm_rstd(0, 1)
            x1_b3_sum(1)

            def slot(s, b, tail, front):
                c = Counts(pool, s)
                stored = 16 * s if isinstance(s, int) else pool.snap(16 * s)
                norm_rstd(1, c.att)
                if front:
                    front_adj_sum(c.front, 1 - b)
                x2_bout_sum(c.att, b)
                if tail:
                    norm_rstd(2, c.tail)
                if front:
                    norm_rstd(0, c.front)
                    x1_b3_sum(c.front, c.att)
                if tail:
                    tail_out(c.tail)
                    tail_norm(c.tail, 1 - b, stored)
                if front:
                    front_extra(c.front, 1 - b, c.two[0])

            slots(pool, slot)
            norm_rstd(2, G)
            tail_out(G)
            tail_norm(G, 1, 16 * G)

        @block.scalar
        def _(act):
            def copy(dst, src, scale=1.0):
                return nc.scalar.activation(dst, src, ACT.Copy, scale=scale)

            act.wait_ge(pe_w, 1)
            copy(w0[0][:, :, :], bank_f[:, 0:2, :]).then_inc(act_w, 1)
            act.wait_ge(pe_w, 2)
            copy(w3[0][:, :, :], bank_d[:, :, 0:L3C]).then_inc(act_w, 1)
            act.wait_ge(dma_weights, 16 * WEIGHT_DMAS)
            copy(w123[0][:, :, :, :], w123_raw[:, :, :, :]).then_inc(act_w, 1)
            for k in range(FT):
                last = copy(wqkv[0][:, k].rearrange("p i (h d) -> p i h d", d=D),
                            wqkv_raw[:, k].rearrange("p (h i d) -> p i h d", i=3, d=D))
            last.then_inc(act_w, 1)
            copy(wout[0][:, :, :], wout_raw[:, :, :]).then_inc(act_w, 1)
            act.wait_ge(dma_biases, 16 * BIAS_DMAS)

            def front_mask(n, b, loaded, before=0):
                act.wait_ge(dma_graph[b], loaded)
                reuse(act, pe_mask2, before)
                copy(mask_row[:, :], mask_u8[:, b]).then_inc(act_mask_row, 1)

            def front_mask2(n, b, before=0, scores_before=0):
                act.wait_ge(pe_mask2, n)
                reuse(act, pool_extra, before)
                copy(mask2[:, :, :], halves(bank_f[:, 0])).then_inc(act_mask2, 1)
                for i in range(NT):
                    reuse(act, dve_scores[1][i], scores_before)
                nc.scalar.activation(minus_big[:, b], halves(bank_f[:, 0]), ACT.Copy, bias=-BIG, scale=BIG) \
                    .then_inc(act_minus_big, 1)

            def front_x(n):
                act.wait_ge(pe_xT, n)
                copy(fT[0][:, :, :], halves(bank_f[:, 1])).then_inc(act_xT, 1)

            def front_adj_t(n, b, before=0):
                act.wait_ge(pe_adjT, n)
                reuse(act, pe_adjk, before)
                copy(adjT[0][:, b], halves(bank_f[:, 2])).then_inc(act_adjT, 1)

            def front_from_adj(n, b, loaded, before=0):
                act.wait_ge(dma_graph[b], loaded)
                reuse(act, pool_extra, before)
                for t in range(NT):
                    last = nc.scalar.activation(adj_junk[:, t], adj_sb[:, b, t], ACT.Copy, accum_out=deg[:, t:t + 1])
                last.then_inc(act_deg, 1)
                nc.scalar.activation(exp_adj[:, :, :], adj_sb[:, b], ACT.Exp, scale=-1.0).then_inc(act_exp_adj, 1)

            def front_sup0(n):
                act.wait_ge(pe_proj0, n)
                copy(sup[0][:, :, :], bank_f[:, 0:2, F:2 * F]).then_inc(act_sup0, 1)

            def front_self(n):
                act.wait_ge(dve_sup0, n)
                copy(self_part[:, :, :], bank_f[:, 0:2, 0:F]).then_inc(act_self, 1)

            def hi(dst, bank, ready, n, done):
                act.wait_ge(ready, n)
                copy(dst, halves(bank)).then_inc(done, 1)

            def front_hidden(layer, n, bank, bias):
                act.wait_ge(pe_hid[layer], n)
                for h in range(FT):
                    last = nc.scalar.activation(hid[:, h], bank[:, h * N:(h + 1) * N], ACT.Relu,
                                                bias=bias[:, h:h + 1])
                last.then_inc(act_hid[layer], 1)
                act.wait_ge(act_hid[layer], n)
                copy(hidT[0][:, :, :], hid[:, :, :]).then_inc(act_hid_hi[layer], 1)

            def values(n):
                act.wait_ge(pe_v, n)
                copy(v_sb[:, :, :], bank_d[:, :, :], scale=MIX).then_inc(act_v, 1)

            def qk(p, c):
                act.wait_ge(pe_qk[p % 2], c.pair(p))
                copy(qT[0][:, p % 2], bank_q[:, 0:N])
                copy(kTz[0][0:D, p % 2, 0], bank_q[0:D, N:2 * N])
                copy(kTz[0][D:P, p % 2, 1], bank_q[D:P, N:2 * N]).then_inc(act_qk[p % 2], 1)

            def exps(p, i, c):
                act.wait_ge(dve_scores[p % 2][i], c.pair(p))
                for h in range(2):
                    last = nc.scalar.activation(prob[:, p % 2, i, h], prob[:, p % 2, i, h], ACT.Exp,
                                                bias=shift[:, p % 2, h, i:i + 1], scale=-1.0,
                                                accum_out=psum_exp[:, p % 2, h, i:i + 1])
                last.then_inc(act_exp[p % 2][i], 1)

            def probs_t(p, h, c):
                act.wait_ge(pe_probT[p % 2][h], c.pair(p))
                if h == 0:
                    reuse(act, pe_pv[p % 2], c.pair(p, 1))
                copy(probT[:, p % 2, h], halves(bank_t[:, :])).then_inc(act_probT[p % 2][h], 1)

            def out_t(p, c):
                act.wait_ge(pe_pv[p % 2], c.pair(p))
                copy(oT[0][:, p], bank_o[:, 0:N]).then_inc(act_oT[p % 2], 1)

            def tail_qkv(n):
                act.wait_ge(pe_proj3, n)
                copy(qkv3[:, :, :], bank_d[:, :, 0:L3C]).then_inc(act_qkv3, 1)

            def tail_exp(n):
                act.wait_ge(dve_gate_shift, n)
                nc.scalar.activation(gate_exp[:, :], bank_o[0:1, 0:N], ACT.Exp, bias=gate_shift[:, :],
                                     accum_out=gate_sum[:, :]).then_inc(act_gate_exp, 1)

            def tail_col(n):
                act.wait_ge(pe_gate_col, n)
                copy(gate_col[:, :], bank_o[:, 0:NT]).then_inc(act_gate_col, 1)

            front_mask(1, 0, 48)
            front_from_adj(1, 0, 48)
            front_x(1)
            front_mask2(1, 0)
            front_adj_t(1, 0)
            front_sup0(1)
            front_self(1)
            hi(fT[0][:, :, :], bank_f[:, 0], pe_x1T, 1, act_x1T)
            hi(sup[0][:, :, :], bank_f[:, 1], pe_sup[0], 1, act_sup[0])
            front_hidden(0, 1, bank_f[:, 2], b1_col)
            hi(sup[0][:, :, :], bank_f[:, 0], pe_sup[1], 1, act_sup[1])
            front_hidden(1, 1, bank_f[:, 1], b2_col)
            hi(sup[0][:, :, :], bank_f[:, 2], pe_sup[2], 1, act_sup[2])

            def slot(s, b, tail, front):
                c = Counts(act, s)
                if front:
                    half = (s + 3) // 2 if isinstance(s, int) else None
                    loaded = 48 * half if half is not None else act.snap(24 * (s + (3 if b else 2)))
                if front:
                    front_mask(c.front, 1 - b, loaded, c.att)
                    front_from_adj(c.front, 1 - b, loaded, c.att)
                    front_mask2(c.front, 1 - b, c.att, c.two[0])
                    front_x(c.front)
                hi(x2T[0][:, :, :], bank_q[:, :], pe_x2T, c.att, act_x2T)
                if front:
                    front_sup0(c.front)
                if tail:
                    hi(x3T[0][:, :, :], bank_o[:, :], pe_x3T, c.tail, act_x3T)
                values(c.att)
                qk(0, c)
                if tail:
                    tail_qkv(c.tail)
                qk(1, c)
                if front:
                    front_adj_t(c.front, 1 - b, c.tail)
                    front_self(c.front)
                exps(0, 0, c)
                qk(2, c)
                exps(0, 1, c)
                exps(1, 0, c)
                if front:
                    hi(fT[0][:, :, :], bank_f[:, 0], pe_x1T, c.front, act_x1T)
                qk(3, c)
                probs_t(0, 0, c)
                exps(1, 1, c)
                if front:
                    hi(sup[0][:, :, :], bank_f[:, 1], pe_sup[0], c.front, act_sup[0])
                probs_t(0, 1, c)
                if tail:
                    tail_exp(c.tail)
                probs_t(1, 0, c)
                exps(2, 1, c)
                if tail:
                    tail_col(c.tail)
                if front:
                    front_hidden(0, c.front, bank_f[:, 2], b1_col)
                exps(2, 0, c)
                out_t(0, c)
                probs_t(1, 1, c)
                exps(3, 1, c)
                if front:
                    hi(sup[0][:, :, :], bank_f[:, 0], pe_sup[1], c.front, act_sup[1])
                probs_t(2, 0, c)
                exps(3, 0, c)
                probs_t(2, 1, c)
                out_t(1, c)
                if front:
                    front_hidden(1, c.front, bank_f[:, 1], b2_col)
                probs_t(3, 0, c)
                out_t(2, c)
                probs_t(3, 1, c)
                if front:
                    hi(sup[0][:, :, :], bank_f[:, 2], pe_sup[2], c.front, act_sup[2])
                out_t(3, c)

            slots(act, slot)
            hi(x3T[0][:, :, :], bank_o[:, :], pe_x3T, G, act_x3T)
            tail_qkv(G)
            tail_exp(G)
            tail_col(G)

        @block.vector
        def _(dve):
            V = nc.vector

            def f32(ap):
                return ap.bitcast(F32)

            def lo(dst, src, hi_part):
                return V.tensor_tensor(dst, src, f32(hi_part), ALU.subtract)

            for part in range(2):
                V.memset(f32(kTz[part][D:P, :, 0]), 0.0)
                V.memset(f32(kTz[part][0:D, :, 1]), 0.0).then_inc(dve_zero, 1)
            dve.wait_ge(act_w, 1)
            lo(w0[1][:, :, :], bank_f[:, 0:2, :], w0[0][:, :, :]).then_inc(dve_w, 1)
            dve.wait_ge(act_w, 2)
            lo(w3[1][:, :, :], bank_d[:, :, 0:L3C], w3[0][:, :, :]).then_inc(dve_w, 1)
            dve.wait_ge(act_w, 3)
            lo(w123[1][:, :, :, :], w123_raw[:, :, :, :], w123[0][:, :, :, :]).then_inc(dve_w, 1)
            dve.wait_ge(act_w, 4)
            for k in range(FT):
                for i in range(3):
                    last = lo(wqkv[1][:, k, i].rearrange("p (h d) -> p h d", d=D),
                              wqkv_raw[:, k].rearrange("p (h i d) -> p i h d", i=3, d=D)[:, i],
                              wqkv[0][:, k, i].rearrange("p (h d) -> p h d", d=D))
            last.then_inc(dve_w, 1)
            dve.wait_ge(act_w, 5)
            lo(wout[1][:, :, :], wout_raw[:, :, :], wout[0][:, :, :]).then_inc(dve_w, 1)

            def split(parts, src, ready, n, done):
                dve.wait_ge(ready, n)
                lo(parts[1], src, parts[0]).then_inc(done, 1)

            def fixed_wait():
                dve.wait_ge(dve_zero, 2)

            def norm_stats(k, src, ready, n):
                dve.wait_ge(ready, n)
                for t in range(NT):
                    last = V.bn_stats(out=bn[:, k, t], in_=src[:, t])
                last.then_inc(dve_bn[k], 1)
                fixed_wait()
                dve.wait_ge(dve_bn[k], n)
                for t in range(NT):
                    last = V.bn_aggr(out=mv[:, k, t], in_=bn[:, k, t])
                last.then_inc(dve_mv[k], 1)

            def norm_apply(k, src, dst, n, done):
                dve.wait_ge(pool_rstd[k], n)
                for t in range(NT):
                    last = V.tensor_scalar(dst[:, t], src[:, t], mv[:, k, t, 0:1], rstd[:, k, t:t + 1],
                                           ALU.subtract, ALU.mult)
                last.then_inc(done, 1)

            def front_x(n):
                split([a[:, :, :] for a in fT], halves(bank_f[:, 1]), act_xT, n, dve_xT)

            def front_adj_t(n, b):
                split([a[:, b] for a in adjT], halves(bank_f[:, 2]), act_adjT, n, dve_adjT)

            def front_degrees(n):
                dve.wait_ge(act_deg, n)
                V.tensor_scalar(rdeg[:, :], deg[:, :], DEG_EPS, None, ALU.max).then_inc(dve_deg, 1)
                dve.wait_ge(dve_deg, n)
                V.reciprocal(rdeg[:, :], rdeg[:, :]).then_inc(dve_rdeg, 1)

            def front_sup0(n):
                split([a[:, :, :] for a in sup], bank_f[:, 0:2, F:2 * F], act_sup0, n, dve_sup0)

            def front_agg(n, b):
                dve.wait_ge(pe_agg, n)
                dve.wait_ge(act_self, n)
                dve.wait_ge(dve_rdeg, n)
                for t in range(NT):
                    last = V.scalar_tensor_tensor(out=x1_pre[:, t], in0=bank_f[:, 2, t * F:(t + 1) * F],
                                                  scalar=rdeg[:, t:t + 1], in1=self_part[:, t],
                                                  op0=ALU.mult, op1=ALU.add)
                last.then_inc(dve_agg, 1)
                dve.wait_ge(dve_agg, n)
                V.scalar_tensor_tensor(out=x1_pre[:, :, :], in0=x1_pre[:, :, :], scalar=0.0, in1=x_sb[:, b],
                                       op0=ALU.max, op1=ALU.add).then_inc(dve_x1_pre, 1)
                norm_stats(0, x1_pre, dve_x1_pre, n)

            def front_hidden(layer, n):
                split([a[:, :, :] for a in hidT], hid[:, :, :], act_hid_hi[layer], n, dve_hid[layer])

            def front_out(n):
                dve.wait_ge(pe_gcn, n)
                dve.wait_ge(pool_x1_b3, n)
                V.tensor_tensor(x2_pre[:, :, :], halves(bank_q[:, :]), x1_b3[:, :, :], ALU.add) \
                    .then_inc(dve_x2_pre, 1)
                norm_stats(1, x2_pre, dve_x2_pre, n)

            def qk(p, c):
                dve.wait_ge(act_qk[p % 2], c.pair(p))
                lo(qT[1][:, p % 2], bank_q[:, 0:N], qT[0][:, p % 2])
                lo(kTz[1][0:D, p % 2, 0], bank_q[0:D, N:2 * N], kTz[0][0:D, p % 2, 0])
                lo(kTz[1][D:P, p % 2, 1], bank_q[D:P, N:2 * N], kTz[0][D:P, p % 2, 1]).then_inc(dve_qk[p % 2], 1)

            def scores(p, i, c, b, first):
                fixed_wait()
                if first:
                    if p == 0:
                        dve.wait_ge(act_minus_big, c.att)
                    reuse(dve, pe_probT[p % 2][1], c.pair(p, 1))
                dve.wait_ge(pe_scores[p % 2][i], c.pair(p))
                for h in range(2):
                    last = V.tensor_tensor_reduce(
                        out=prob[:, p % 2, i, h], in0=bank_d[:, i, h * N:(h + 1) * N],
                        in1=minus_big[:, b, i], scale=-QK_SCALE, scalar=3.0e38, op0=ALU.add, op1=ALU.min,
                        accum_out=shift[:, p % 2, h, i:i + 1])
                last.then_inc(dve_scores[p % 2][i], 1)

            def probs(p, h, c, b, first):
                if first:
                    for i in range(NT):
                        dve.wait_ge(act_exp[p % 2][i], c.pair(p))
                    V.reciprocal(rsum[:, p % 2], psum_exp[:, p % 2]).then_inc(dve_rsum[p % 2], 1)
                    dve.wait_ge(dve_rsum[p % 2], c.pair(p))
                for i in range(NT):
                    last = V.scalar_tensor_tensor(out=prob[:, p % 2, i, h], in0=prob[:, p % 2, i, h],
                                                  scalar=rsum[:, p % 2, h, i:i + 1], in1=extra[:, b, i],
                                                  op0=ALU.mult, op1=ALU.add)
                last.then_inc(dve_prob[p % 2][h], 1)

            def out_t(p, c):
                dve.wait_ge(act_oT[p % 2], c.pair(p))
                lo(oT[1][:, p], bank_o[:, 0:N], oT[0][:, p]).then_inc(dve_oT[p % 2], 1)

            def attention_out(n, b):
                dve.wait_ge(pe_y, n)
                dve.wait_ge(pool_x2_bout, n)
                V.tensor_tensor(x3_pre[:, :, :], halves(bank_t[:, :]), x2_bout[:, b], ALU.add) \
                    .then_inc(dve_x3_pre, 1)
                norm_stats(2, x3_pre, dve_x3_pre, n)

            def tail_k(n):
                dve.wait_ge(act_qkv3, n)
                V.tensor_copy(k3[:, :, 0], qkv3[:, :, D:2 * D]).then_inc(dve_k3_hi, 1)
                dve.wait_ge(dve_k3_hi, n)
                lo(k3[:, :, 1], qkv3[:, :, D:2 * D], k3[:, :, 0]).then_inc(dve_k3, 1)

            def tail_gate(n):
                dve.wait_ge(pe_adjk, n)
                for t in range(NT):
                    last = V.tensor_tensor_reduce(
                        out=gate_junk[:, t], in0=bank_o[:, t * P:(t + 1) * P].rearrange("p (a d) -> p a d", a=2),
                        in1=qkv3[:, t, 0:D].unsqueeze(1).broadcast_to([P, 2, D]), scale=QK_SCALE, scalar=0.0,
                        op0=ALU.mult, op1=ALU.add, accum_out=gate[:, t:t + 1])
                last.then_inc(dve_gate, 1)

            def tail_max(n):
                dve.wait_ge(pe_gate_row, n)
                V.tensor_reduce(gate_max[:, :], bank_o[0:1, 0:N], AX.X, ALU.max).then_inc(dve_gate_max, 1)
                dve.wait_ge(dve_gate_max, n)
                V.tensor_scalar(gate_shift[:, :], gate_max[:, :], -1.0, None, ALU.mult).then_inc(dve_gate_shift, 1)

            def tail_prob(n):
                dve.wait_ge(act_gate_exp, n)
                V.reciprocal(gate_rsum[:, :], gate_sum[:, :]).then_inc(dve_gate_rsum, 1)
                dve.wait_ge(dve_gate_rsum, n)
                V.tensor_scalar(gate_prob[:, :], gate_exp[:, :], gate_rsum[:, :], None, ALU.mult) \
                    .then_inc(dve_gate_prob, 1)

            front_x(1)
            front_adj_t(1, 0)
            front_degrees(1)
            front_sup0(1)
            front_agg(1, 0)
            norm_apply(0, x1_pre, x1, 1, dve_x[0])
            split([a[:, :, :] for a in fT], halves(bank_f[:, 0]), act_x1T, 1, dve_x1T)
            split([a[:, :, :] for a in sup], halves(bank_f[:, 1]), act_sup[0], 1, dve_sup[0])
            front_hidden(0, 1)
            split([a[:, :, :] for a in sup], halves(bank_f[:, 0]), act_sup[1], 1, dve_sup[1])
            front_hidden(1, 1)
            split([a[:, :, :] for a in sup], halves(bank_f[:, 2]), act_sup[2], 1, dve_sup[2])

            def slot(s, b, tail, front):
                c = Counts(dve, s)
                front_out(c.att)
                if front:
                    front_x(c.front)
                norm_apply(1, x2_pre, x2, c.att, dve_x[1])
                split([a[:, :, :] for a in x2T], halves(bank_q[:, :]), act_x2T, c.att, dve_x2T)
                if tail:
                    attention_out(c.tail, 1 - b)
                if front:
                    front_sup0(c.front)
                if tail:
                    norm_apply(2, x3_pre, x3, c.tail, dve_x[2])
                    split([a[:, :, :] for a in x3T], halves(bank_o[:, :]), act_x3T, c.tail, dve_x3T)
                qk(0, c)
                if tail:
                    tail_k(c.tail)
                if front:
                    front_degrees(c.front)
                qk(1, c)
                if front:
                    front_adj_t(c.front, 1 - b)
                scores(0, 0, c, b, first=True)
                if tail:
                    tail_gate(c.tail)
                scores(0, 1, c, b, first=False)
                if front:
                    front_agg(c.front, 1 - b)
                qk(2, c)
                scores(1, 0, c, b, first=True)
                if front:
                    norm_apply(0, x1_pre, x1, c.front, dve_x[0])
                probs(0, 0, c, b, first=True)
                scores(1, 1, c, b, first=False)
                if front:
                    split([a[:, :, :] for a in fT], halves(bank_f[:, 0]), act_x1T, c.front, dve_x1T)
                probs(0, 1, c, b, first=False)
                if tail:
                    tail_max(c.tail)
                probs(1, 0, c, b, first=True)
                if front:
                    split([a[:, :, :] for a in sup], halves(bank_f[:, 1]), act_sup[0], c.front, dve_sup[0])
                scores(2, 1, c, b, first=True)
                if tail:
                    tail_prob(c.tail)
                qk(3, c)
                probs(1, 1, c, b, first=False)
                scores(2, 0, c, b, first=False)
                if front:
                    front_hidden(0, c.front)
                scores(3, 1, c, b, first=True)
                probs(2, 0, c, b, first=True)
                out_t(0, c)
                probs(2, 1, c, b, first=False)
                scores(3, 0, c, b, first=False)
                if front:
                    split([a[:, :, :] for a in sup], halves(bank_f[:, 0]), act_sup[1], c.front, dve_sup[1])
                if tail:
                    norm_stats(3, x4_pre, pool_x4_pre, c.tail)
                probs(3, 0, c, b, first=True)
                out_t(1, c)
                probs(3, 1, c, b, first=False)
                if front:
                    front_hidden(1, c.front)
                out_t(2, c)
                if front:
                    split([a[:, :, :] for a in sup], halves(bank_f[:, 2]), act_sup[2], c.front, dve_sup[2])
                out_t(3, c)

            slots(dve, slot)
            attention_out(G, 1)
            norm_apply(2, x3_pre, x3, G, dve_x[2])
            split([a[:, :, :] for a in x3T], halves(bank_o[:, :]), act_x3T, G, dve_x3T)
            tail_k(G)
            tail_gate(G)
            tail_max(G)
            tail_prob(G)
            norm_stats(3, x4_pre, pool_x4_pre, G)

        @block.tensor
        def _(pe):
            mm = nc.tensor.matmul
            PASSES = ((0, 0), (0, 1), (1, 0))

            def product(dst, terms):
                count = len(terms) * len(PASSES)
                n = 0
                for left, right in terms:
                    for a, b in PASSES:
                        last = mm(dst, left[a], right[b], start=n == 0, stop=n == count - 1)
                        n += 1
                return last

            def cut(parts, *index):
                return [a[index] for a in parts]

            A = slice(None)

            def block_of(i, size=P):
                return slice(i * size, (i + 1) * size)

            def transpose_tiles(bank, src):
                for r in range(2):
                    for t in range(2):
                        last = nc.tensor.transpose(bank[:, r * N + t * P:r * N + (t + 1) * P],
                                                   src[:, t, block_of(r)], ident[:, :])
                return last

            pe.wait_ge(pool_ident, 2)
            pe.wait_ge(dma_weights, 16 * WEIGHT_DMAS)
            for k in range(FT):
                for part in range(2):
                    for o in range(FT):
                        last = nc.tensor.transpose(bank_f[:, k, part * F + o * P:part * F + (o + 1) * P],
                                                   w0_raw[:, o, part * F + k * P:part * F + (k + 1) * P],
                                                   ident[:, :])
            last.then_inc(pe_w, 1)
            for k in range(FT):
                nc.tensor.transpose(bank_d[:, k, 0:P], wqk3_raw[:, block_of(k)], ident[:, :])
                for o in range(FT):
                    last = nc.tensor.transpose(bank_d[:, k, P + o * P:P + (o + 1) * P],
                                               wv3_raw[:, o, block_of(k)], ident[:, :])
            last.then_inc(pe_w, 1)
            pe.wait_ge(dve_w, TILES_W)
            pe.wait_ge(dve_zero, 2)

            def mask_product(n, before=0):
                pe.wait_ge(act_mask_row, n)
                reuse(pe, dve_sup[1], before)
                for t in range(NT):
                    last = mm(bank_f[:, 0, t * N:(t + 1) * N], mask_row[:, block_of(t)], mask_row[:, :],
                              start=True, stop=True)
                last.then_inc(pe_mask2, 1)

            def x_transpose(n, b, loaded, before=0):
                pe.wait_ge(dma_graph[b], loaded)
                reuse(pe, act_hid[1], before)
                transpose_tiles(bank_f[:, 1], x_sb[:, b]).then_inc(pe_xT, 1)

            def adj_transpose(n, b, before=0):
                reuse(pe, dve_sup[2], before)
                transpose_tiles(bank_f[:, 2], adj_sb[:, b]).then_inc(pe_adjT, 1)

            def front_project(n):
                pe.wait_ge(dve_xT, n)
                pe.wait_ge(act_minus_big, n)
                for t in range(NT):
                    last = product(bank_f[:, t, :], [(cut(fT, A, k, block_of(t)), cut(w0, A, k)) for k in range(FT)])
                last.then_inc(pe_proj0, 1)

            def adj_times_support(bank, b):
                for t in range(NT):
                    last = product(bank[:, t * F:(t + 1) * F],
                                   [(cut(adjT, A, b, k, block_of(t)), cut(sup, A, k)) for k in range(NT)])
                return last

            def front_aggregate(n, b):
                pe.wait_ge(dve_sup0, n)
                pe.wait_ge(dve_adjT, n)
                adj_times_support(bank_f[:, 2], b).then_inc(pe_agg, 1)

            def front_x1_transpose(n):
                pe.wait_ge(dve_x[0], n)
                transpose_tiles(bank_f[:, 0], x1).then_inc(pe_x1T, 1)

            def front_support(layer, n, bank, src, ready):
                pe.wait_ge(ready, n)
                for t in range(NT):
                    last = product(bank[:, t * F:(t + 1) * F],
                                   [(cut(src, A, k, block_of(t)), cut(w123, A, layer, k)) for k in range(FT)])
                last.then_inc(pe_sup[layer], 1)

            def front_hidden(layer, n, bank, b):
                pe.wait_ge(dve_sup[layer], n)
                for h in range(FT):
                    last = product(bank[:, h * N:(h + 1) * N],
                                   [(cut(sup, A, k, block_of(h)), cut(adjT, A, b, k)) for k in range(NT)])
                last.then_inc(pe_hid[layer], 1)

            def front_out(n, b, before):
                pe.wait_ge(dve_sup[2], n)
                reuse(pe, dve_qk[1], before)
                adj_times_support(bank_q[:, :], b).then_inc(pe_gcn, 1)

            def x2_transpose(n):
                pe.wait_ge(dve_x[1], n)
                transpose_tiles(bank_q[:, :], x2).then_inc(pe_x2T, 1)

            def values(n):
                pe.wait_ge(dve_x2T, n)
                for t in range(NT):
                    last = product(bank_d[:, t, :],
                                   [(cut(x2T, A, k, block_of(t)), cut(wqkv, A, k, 2)) for k in range(FT)])
                last.then_inc(pe_v, 1)

            def qk(p, c):
                if p:
                    pe.wait_ge(dve_qk[(p - 1) % 2], c.pair(p - 1))
                else:
                    pe.wait_ge(dve_x2T, c.att)
                for i in range(2):
                    last = product(bank_q[:, i * N:(i + 1) * N],
                                   [(cut(wqkv, A, k, i, block_of(p)), cut(x2T, A, k)) for k in range(FT)])
                last.then_inc(pe_qk[p % 2], 1)

            def scores(p, i, c, tail, first):
                if first:
                    pe.wait_ge(dve_qk[p % 2], c.pair(p))
                if p:
                    pe.wait_ge(dve_scores[(p - 1) % 2][i], c.pair(p - 1))
                elif first and tail:
                    pe.wait_ge(act_qkv3, c.tail)
                product(bank_d[:, i, :],
                        [(cut(qT, A, p % 2, block_of(i)),
                          [a[:, p % 2].rearrange("p h n -> p (h n)") for a in kTz])]) \
                    .then_inc(pe_scores[p % 2][i], 1)

            def probs_t(p, h, c, tail):
                pe.wait_ge(dve_prob[p % 2][h], c.pair(p))
                if h:
                    pe.wait_ge(act_probT[p % 2][0], c.pair(p))
                elif p:
                    pe.wait_ge(act_probT[(p - 1) % 2][1], c.pair(p - 1))
                elif tail:
                    pe.wait_ge(dve_x3_pre, c.tail)
                transpose_tiles(bank_t[:, :], prob[:, p % 2, :, h]).then_inc(pe_probT[p % 2][h], 1)

            def attend(p, c, tail):
                pe.wait_ge(act_probT[p % 2][1], c.pair(p))
                if p:
                    pe.wait_ge(dve_oT[(p - 1) % 2], c.pair(p - 1))
                else:
                    pe.wait_ge(act_v, c.att)
                    if tail:
                        pe.wait_ge(act_gate_col, c.tail)
                for k in range(NT):
                    for h in range(2):
                        last = mm(bank_o[h * D:(h + 1) * D, 0:N], v_sb[:, k, (2 * p + h) * D:(2 * p + h + 1) * D],
                                  probT[:, p % 2, h, k], start=k == 0, stop=k == NT - 1)
                last.then_inc(pe_pv[p % 2], 1)

            def project_out(pairs):
                pe.wait_ge(dve_oT[0], pairs)
                pe.wait_ge(dve_oT[1], pairs)
                for t in range(NT):
                    last = product(bank_t[:, t * F:(t + 1) * F],
                                   [(cut(oT, A, p, block_of(t)), cut(wout, A, p)) for p in range(PAIRS)])
                last.then_inc(pe_y, 1)

            def tail_transpose(n):
                pe.wait_ge(dve_x[2], n)
                transpose_tiles(bank_o[:, :], x3).then_inc(pe_x3T, 1)

            def tail_project(n, after_v):
                pe.wait_ge(dve_x3T, n)
                reuse(pe, act_v, after_v)
                for t in range(NT):
                    last = product(bank_d[:, t, 0:L3C],
                                   [(cut(x3T, A, k, block_of(t)), cut(w3, A, k)) for k in range(FT)])
                last.then_inc(pe_proj3, 1)

            def tail_adj_k(n, b):
                pe.wait_ge(dve_k3, n)
                for t in range(NT):
                    at = t * P
                    for k in range(NT):
                        mm(bank_o[:, at:at + 2 * D], adjT[0][:, b, k, block_of(t)],
                           k3[:, k].rearrange("p a d -> p (a d)"), start=k == 0, stop=False)
                    for k in range(NT):
                        last = mm(bank_o[:, at:at + D], adjT[1][:, b, k, block_of(t)], k3[:, k, 0],
                                  start=False, stop=k == NT - 1)
                last.then_inc(pe_adjk, 1)

            def tail_gate_row(n):
                pe.wait_ge(dve_gate, n)
                for t in range(NT):
                    last = nc.tensor.transpose(bank_o[0:1, t * P:(t + 1) * P], gate[:, t:t + 1], ident[:, :])
                last.then_inc(pe_gate_row, 1)

            def tail_gate_col(n):
                pe.wait_ge(dve_gate_prob, n)
                for t in range(NT):
                    last = mm(bank_o[:, t:t + 1], gate_prob[:, block_of(t)], one[:, :], start=True, stop=True)
                last.then_inc(pe_gate_col, 1)

            x_transpose(1, 0, 48)
            mask_product(1)
            adj_transpose(1, 0)
            front_project(1)
            front_aggregate(1, 0)
            front_x1_transpose(1)
            front_support(0, 1, bank_f[:, 1], fT, dve_x1T)
            front_hidden(0, 1, bank_f[:, 2], 0)
            front_support(1, 1, bank_f[:, 0], hidT, dve_hid[0])
            front_hidden(1, 1, bank_f[:, 1], 0)
            front_support(2, 1, bank_f[:, 2], hidT, dve_hid[1])

            def slot(s, b, tail, front):
                c = Counts(pe, s)
                if front:
                    half = (s + 3) // 2 if isinstance(s, int) else None
                    loaded = 48 * half if half is not None else pe.snap(24 * (s + (3 if b else 2)))
                if front:
                    x_transpose(c.front, 1 - b, loaded, c.att)
                front_out(c.att, b, c.two[0])
                if front:
                    mask_product(c.front, c.att)
                if tail:
                    project_out(c.two[0])
                if front:
                    adj_transpose(c.front, 1 - b, c.att)
                x2_transpose(c.att)
                if front:
                    front_project(c.front)
                values(c.att)
                if tail:
                    tail_transpose(c.tail)
                qk(0, c)
                if tail:
                    tail_project(c.tail, c.att)
                qk(1, c)
                if tail:
                    tail_adj_k(c.tail, 1 - b)
                scores(0, 1, c, tail, first=True)
                scores(0, 0, c, tail, first=False)
                if front:
                    front_aggregate(c.front, 1 - b)
                qk(2, c)
                scores(1, 1, c, tail, first=True)
                scores(1, 0, c, tail, first=False)
                if tail:
                    tail_gate_row(c.tail)
                qk(3, c)
                if front:
                    front_x1_transpose(c.front)
                probs_t(0, 0, c, tail)
                if front:
                    front_support(0, c.front, bank_f[:, 1], fT, dve_x1T)
                probs_t(0, 1, c, tail)
                scores(2, 1, c, tail, first=True)
                probs_t(1, 0, c, tail)
                if front:
                    front_hidden(0, c.front, bank_f[:, 2], 1 - b)
                if tail:
                    tail_gate_col(c.tail)
                scores(2, 0, c, tail, first=False)
                scores(3, 1, c, tail, first=True)
                probs_t(1, 1, c, tail)
                attend(0, c, tail)
                scores(3, 0, c, tail, first=False)
                if front:
                    front_support(1, c.front, bank_f[:, 0], hidT, dve_hid[0])
                probs_t(2, 0, c, tail)
                attend(1, c, tail)
                probs_t(2, 1, c, tail)
                if front:
                    front_hidden(1, c.front, bank_f[:, 1], 1 - b)
                probs_t(3, 0, c, tail)
                attend(2, c, tail)
                probs_t(3, 1, c, tail)
                if front:
                    front_support(2, c.front, bank_f[:, 2], hidT, dve_hid[1])
                attend(3, c, tail)

            slots(pe, slot)
            project_out(2 * G)
            tail_transpose(G)
            tail_project(G, 0)
            tail_adj_k(G, 1)
            tail_gate_row(G)
            tail_gate_col(G)


_INS = ["x", "adj", "nodemask", "L0_gnn_W", "L1_gnn_W1", "L1_gnn_b1", "L1_gnn_W2", "L1_gnn_b2", "L1_gnn_W3",
        "L1_gnn_b3", "L2_gnn_W_qkv", "L2_gnn_W_out", "L2_gnn_b_out", "L3_gnn_W_qk", "L3_gnn_W_v"]


def kernel(**inputs):
    import numpy as _np
    import concourse.bacc as _bacc
    from concourse import mybir as _mybir
    from concourse.bass_utils import run_bass_kernel_spmd as _run

    nc = _bacc.Bacc("TRN2", target_bir_lowering=False, num_devices=1)
    arrays, args = {}, []
    for name in _INS:
        a = _np.ascontiguousarray(inputs[name])
        arrays[f"in_{name}"] = a
        args.append(nc.dram_tensor(f"in_{name}", a.shape, _mybir.dt.from_np(a.dtype), kind="ExternalInput").ap())
    args.append(nc.dram_tensor("out_0", inputs["x"].shape, F32, kind="ExternalOutput").ap())
    graph_blocks_kernel(nc, *args)
    r = _run(nc, [arrays], core_ids=[0])
    return r.results[0]["out_0"]
```

```python
from contextlib import ExitStack

import numpy as np
import concourse.bass as bass
from concourse import mybir

F32 = mybir.dt.float32
F32R = mybir.dt.float32r
ALU = mybir.AluOpType
ACT = mybir.ActivationFunctionType
AX = mybir.AxisListType


def graph_blocks_kernel(nc, x, adj, nodemask, L0_W, L1_W1, L1_b1, L1_W2, L1_b2, L1_W3, L1_b3,
                        L2_Wqkv, L2_Wout, L2_bout, L3_Wqk, L3_Wv, out):
    G, N, F = x.shape
    P = 128
    NT = N // P
    FT = F // P
    D = 64
    HEADS = L2_Wout.shape[0] // D
    PAIRS = HEADS // 2
    INNER = HEADS * D
    LN_EPS, DEG_EPS = 1e-5, 1e-6
    MIX = 0.33
    QK_SCALE = D ** -0.5
    BIG = 2.0 ** 100
    L3C = 2 * D + F
    assert (N, F, PAIRS, G % 2) == (256, 256, 4, 0)

    by_node = "g (n p) f -> g p n f"
    x_d, adj_d, out_d = (a.rearrange(by_node, p=P) for a in (x, adj, out))

    ctx = ExitStack()
    with ctx:
        def sb(name, shape, dt=F32):
            return ctx.enter_context(nc.sbuf_tensor(name, shape, dt))

        def sem(name):
            return ctx.enter_context(nc.semaphore(name))

        def sems(name, n=2):
            return [sem(f"{name}_{i}") for i in range(n)]

        w0_raw = sb("w0_raw", [P, F // P, 2 * F])
        w123_raw = sb("w123_raw", [P, 3, FT, F])
        work = sb("work", [P, 2, 2 * NT * 2 * N])
        wqkv_raw = work[:, :, 0:3 * INNER]
        wout_raw = sb("wout_raw", [P, PAIRS, F])
        wqk3_raw = sb("wqk3_raw", [P, F])
        wv3_raw = sb("wv3_raw", [P, FT, F])
        b1_col = sb("b1_col", [P, FT])
        b2_col = sb("b2_col", [P, FT])
        b3_row = sb("b3_row", [P, F])
        bout_row = sb("bout_row", [P, F])
        ident = sb("ident", [P, P])
        one = sb("one", [1, 1])
        minus_half = sb("minus_half", [P, NT])
        eps = sb("eps", [P, NT])
        w0 = [sb(f"w0_{s}", [P, FT, 2 * F], F32R) for s in "hl"]
        w123 = [sb(f"w123_{s}", [P, 3, FT, F], F32R) for s in "hl"]
        wqkv = [sb(f"wqkv_{s}", [P, FT, 3, INNER], F32R) for s in "hl"]
        wout = [sb(f"wout_{s}", [P, PAIRS, F], F32R) for s in "hl"]
        w3 = [sb(f"w3_{s}", [P, FT, L3C], F32R) for s in "hl"]
        x_sb = sb("x_sb", [P, 2, NT, F])
        adj_sb = sb("adj_sb", [P, 2, NT, N])
        mask_u8 = sb("mask_u8", [1, 2, N], nodemask.dtype)
        mask_row = sb("mask_row", [1, N], F32R)
        mask2 = sb("mask2", [P, NT, N])
        exp_adj = sb("exp_adj", [P, NT, N])
        adj_junk = sb("adj_junk", [P, NT, N])
        deg = sb("deg", [P, NT])
        rdeg = sb("rdeg", [P, NT])
        extra = sb("extra", [P, 2, NT, N])
        minus_big = sb("minus_big", [P, 2, NT, N])
        adjT = [sb(f"adjT_{s}", [P, 2, NT, N], F32R) for s in "hl"]
        fT = [sb(f"fT_{s}", [P, FT, N], F32R) for s in "hl"]
        sup = [sb(f"sup_{s}", [P, NT, F], F32R) for s in "hl"]
        self_part = sb("self_part", [P, NT, F])
        x1_pre = sb("x1_pre", [P, NT, F])
        x1 = sb("x1", [P, NT, F])
        x1_b3 = sb("x1_b3", [P, NT, F])
        hid = sb("hid", [P, FT, N])
        hidT = [sb(f"hidT_{s}", [P, FT, N], F32R) for s in "hl"]
        x2_pre = sb("x2_pre", [P, NT, F])
        x2 = sb("x2", [P, NT, F])
        x2_bout = sb("x2_bout", [P, 2, NT, F])
        x2T = [sb(f"x2T_{s}", [P, FT, N], F32R) for s in "hl"]
        v_sb = sb("v_sb", [P, NT, INNER])
        qT = [sb(f"qT_{s}", [P, 2, N], F32R) for s in "hl"]
        kTz = [sb(f"kTz_{s}", [P, 2, 2, N], F32R) for s in "hl"]
        prob = work[:, 0].rearrange("p (a i h j) -> p a i h j", a=2, i=NT, h=2)
        shift = sb("shift", [P, 2, 2, NT])
        psum_exp = sb("psum_exp", [P, 2, 2, NT])
        rsum = sb("rsum", [P, 2, 2, NT])
        probT = work[:, 1].rearrange("p (a h j i) -> p a h j i", a=2, h=2, j=NT)
        oT = [sb(f"oT_{s}", [P, PAIRS, N], F32R) for s in "hl"]
        x3_pre = sb("x3_pre", [P, NT, F])
        x3 = sb("x3", [P, NT, F])
        x3T = [sb(f"x3T_{s}", [P, FT, N], F32R) for s in "hl"]
        qkv3 = sb("qkv3", [P, NT, L3C])
        k3 = sb("k3", [P, NT, 2, D], F32R)
        gate_junk = sb("gate_junk", [P, NT, 2, D])
        gate = sb("gate", [P, NT])
        gate_max = sb("gate_max", [1, 1])
        gate_shift = sb("gate_shift", [1, 1])
        gate_sum = sb("gate_sum", [1, 1])
        gate_rsum = sb("gate_rsum", [1, 1])
        gate_exp = sb("gate_exp", [1, N])
        gate_prob = sb("gate_prob", [1, N])
        gate_col = sb("gate_col", [P, NT])
        x4_pre = sb("x4_pre", [P, NT, F])
        y_sb = sb("y_sb", [P, 2, NT, F])
        bn = sb("bn", [P, 4, NT, 6])
        mv = sb("mv", [P, 4, NT, 2])
        rstd = sb("rstd", [P, 4, NT])

        bank_f = ctx.enter_context(nc.psum_tensor("bank_f", [P, 3, 512], F32))
        bank_d = ctx.enter_context(nc.psum_tensor("bank_d", [P, 2, 512], F32))
        bank_q = ctx.enter_context(nc.psum_tensor("bank_q", [P, 512], F32))
        bank_t = ctx.enter_context(nc.psum_tensor("bank_t", [P, 512], F32))
        bank_o = ctx.enter_context(nc.psum_tensor("bank_o", [P, 512], F32))

        def halves(ap):
            return ap.rearrange("p (a b) -> p a b", a=2)

        dma_w0, dma_w123, dma_w3, dma_wqkv, dma_wout, dma_biases = (
            sem(n) for n in ("dma_w0", "dma_w123", "dma_w3", "dma_wqkv", "dma_wout", "dma_biases"))
        dma_graph = sems("dma_graph")
        dma_out = sem("dma_out")
        pool_const, pool_ident, pool_adj_sum, pool_extra, act_minus_big = (
            sem(n) for n in ("pool_const", "pool_ident", "pool_adj_sum", "pool_extra", "act_minus_big"))
        pool_rstd = sems("pool_rstd", 4)
        pool_var, dve_x = sems("pool_var", 4), sems("dve_x", 3)
        pool_centred, pool_y = sem("pool_centred"), sem("pool_y")
        pool_x1_b3, pool_x2_bout, pool_gate_v, pool_x4_pre = (
            sem(n) for n in ("pool_x1_b3", "pool_x2_bout", "pool_gate_v", "pool_x4_pre"))
        (pe_w, pe_mask2, pe_xT, pe_adjT, pe_proj0, pe_agg, pe_x1T, pe_gcn, pe_x2T, pe_v, pe_y, pe_x3T,
         pe_proj3, pe_adjk, pe_gate_row, pe_gate_col) = (
            sem(n) for n in ("pe_w", "pe_mask2", "pe_xT", "pe_adjT", "pe_proj0", "pe_agg", "pe_x1T", "pe_gcn",
                             "pe_x2T", "pe_v", "pe_y", "pe_x3T", "pe_proj3", "pe_adjk", "pe_gate_row",
                             "pe_gate_col"))
        pe_sup, pe_hid = sems("pe_sup", 3), sems("pe_hid")
        pe_qk, pe_pv = sems("pe_qk"), sems("pe_pv")
        pe_scores = [sems(f"pe_scores{i}_") for i in range(2)]
        pe_probT = [sems(f"pe_probT{i}_") for i in range(2)]
        (act_w, act_mask_row, act_mask2, act_xT, act_adjT, act_deg, act_exp_adj, act_sup0, act_self,
         act_x1T, act_x2T, act_v,
         act_x3T, act_qkv3, act_gate_exp, act_gate_col) = (
            sem(n) for n in ("act_w", "act_mask_row", "act_mask2", "act_xT", "act_adjT", "act_deg",
                             "act_exp_adj", "act_sup0", "act_self",
                             "act_x1T", "act_x2T", "act_v", "act_x3T", "act_qkv3", "act_gate_exp",
                             "act_gate_col"))
        act_sup, act_hid, act_hid_hi = sems("act_sup", 3), sems("act_hid"), sems("act_hid_hi")
        act_qk, act_oT = sems("act_qk"), sems("act_oT")
        act_exp = [sems(f"act_exp{i}_") for i in range(2)]
        act_probT = [sems(f"act_probT{i}_") for i in range(2)]
        (dve_w, dve_zero, dve_xT, dve_adjT, dve_deg, dve_rdeg, dve_sup0, dve_agg, dve_x1_pre, dve_x1T,
         dve_x2_pre, dve_x2T, dve_x3_pre, dve_x3T, dve_k3_hi, dve_k3, dve_gate, dve_gate_max,
         dve_gate_shift, dve_gate_rsum, dve_gate_prob) = (
            sem(n) for n in ("dve_w", "dve_zero", "dve_xT", "dve_adjT", "dve_deg", "dve_rdeg", "dve_sup0",
                             "dve_agg", "dve_x1_pre", "dve_x1T", "dve_x2_pre", "dve_x2T", "dve_x3_pre",
                             "dve_x3T", "dve_k3_hi", "dve_k3", "dve_gate", "dve_gate_max", "dve_gate_shift",
                             "dve_gate_rsum", "dve_gate_prob"))
        dve_sup, dve_hid = sems("dve_sup", 3), sems("dve_hid")
        dve_bn, dve_mv = sems("dve_bn", 4), sems("dve_mv", 4)
        dve_qk, dve_rsum, dve_oT = sems("dve_qk"), sems("dve_rsum"), sems("dve_oT")
        dve_scores = [sems(f"dve_scores{i}_") for i in range(2)]
        dve_prob = [sems(f"dve_prob{i}_") for i in range(2)]

        def reuse(eng, semaphore, n):
            if not isinstance(n, int) or n > 0:
                eng.wait_ge(semaphore, n)

        class Counts:

            def __init__(self, eng, s):
                keep = (lambda v: v) if isinstance(s, int) else eng.snap
                self.tail = keep(s) if not isinstance(s, int) else s
                self.att = keep(s + 1)
                self.front = keep(s + 2)
                self.ahead = keep(s + 3)
                self.two = [keep(2 * s), keep(2 * s + 1), keep(2 * s + 2)]

            def pair(self, p, back=0):
                return self.two[1 + p // 2 - back]

        def loads_done(eng, s, b, further):
            if isinstance(s, int):
                return 48 * ((s + further) // 2 + 1)
            odd = (b + further) % 2
            return eng.snap(24 * (s + further + 2 - odd))

        def slots(eng, slot):
            slot(0, 0, tail=False, front=True, ahead=True)
            with eng.Fori(0, G // 2 - 2) as u:
                slot(2 * u + 1, 1, tail=True, front=True, ahead=True)
                slot(2 * u + 2, 0, tail=True, front=True, ahead=True)
            slot(G - 3, 1, tail=True, front=True, ahead=True)
            slot(G - 2, 0, tail=True, front=True, ahead=False)
            slot(G - 1, 1, tail=True, front=False, ahead=False)

        BIAS_DMAS = 4
        W0, W1, W3TH, W_LAST, W_QKV, W_OUT = 1, 2, 4, 5, 6, 8
        block = ctx.enter_context(nc.Block())

        @block.sync
        def _(sp):
            def load(g, b):
                sp.dma_start(x_sb[:, b], x_d[bass.ds(g, 1)].rearrange("g p n f -> (g p) n f")) \
                    .then_inc(dma_graph[b], 16)
                sp.dma_start(adj_sb[:, b], adj_d[bass.ds(g, 1)].rearrange("g p n f -> (g p) n f")) \
                    .then_inc(dma_graph[b], 16)
                sp.dma_start(mask_u8[:, b], nodemask[bass.ds(g, 1)]).then_inc(dma_graph[b], 16)

            def store(g, b):
                sp.dma_start(out_d[bass.ds(g, 1)].rearrange("g p n f -> (g p) n f"), y_sb[:, b]) \
                    .then_inc(dma_out, 16)

            sp.sem_inc(dma_out, 32)
            load(0, 0)
            sp.dma_start(w0_raw[:, :, :], L0_W.rearrange("(n p) f -> p n f", p=P)).then_inc(dma_w0, 16)
            for i, w in enumerate((L1_W1, L1_W2, L1_W3)):
                sp.dma_start(w123_raw[:, i], w.rearrange("(k p) h -> p k h", p=P)).then_inc(dma_w123, 16)
            sp.dma_start(wqk3_raw[:, :], L3_Wqk).then_inc(dma_w3, 16)
            sp.dma_start(wv3_raw[:, :, :], L3_Wv.rearrange("(n p) f -> p n f", p=P)).then_inc(dma_w3, 16)
            sp.dma_start(wqkv_raw[:, :, :], L2_Wqkv.rearrange("(k p) h -> p k h", p=P)).then_inc(dma_wqkv, 16)
            sp.dma_start(wout_raw[:, :, :], L2_Wout.rearrange("(k p) h -> p k h", p=P)).then_inc(dma_wout, 16)
            sp.dma_start(b1_col[:, :], L1_b1.rearrange("(k p) -> p k", p=P), allow_slow_non_contiguous=True) \
                .then_inc(dma_biases, 16)
            sp.dma_start(b2_col[:, :], L1_b2.rearrange("(k p) -> p k", p=P), allow_slow_non_contiguous=True) \
                .then_inc(dma_biases, 16)
            sp.dma_start(b3_row[:, :], L1_b3.rearrange("(a f) -> a f", a=1).broadcast_to([P, F])) \
                .then_inc(dma_biases, 16)
            sp.dma_start(bout_row[:, :], L2_bout.rearrange("(a f) -> a f", a=1).broadcast_to([P, F])) \
                .then_inc(dma_biases, 16)
            load(1, 1)

            def slot(s, b, tail=True, prefetch=True):
                done = s + 1 if isinstance(s, int) else sp.snap(s + 1)
                if prefetch:
                    g = s + 2 if isinstance(s, int) else sp.snap(s + 2)
                    sp.wait_ge(pool_const, 1)
                    sp.wait_ge(dve_x1_pre, done)
                    sp.wait_ge(pe_adjT, done)
                    sp.wait_ge(pool_adj_sum, done)
                    sp.wait_ge(act_mask_row, done)
                    load(g, b)
                if tail:
                    g = s - 1 if isinstance(s, int) else sp.snap(s - 1)
                    before = 16 * s + 16 if isinstance(s, int) else sp.snap(16 * s + 16)
                    sp.wait_ge(pool_const, 1)
                    sp.wait_ge(pool_y, s if isinstance(s, int) else sp.snap(s + 0))
                    sp.wait_ge(dma_out, before)
                    store(g, 1 - b)

            slot(0, 0, tail=False)
            with sp.Fori(0, G // 2 - 2) as u:
                slot(2 * u + 1, 1)
                slot(2 * u + 2, 0)
            slot(G - 3, 1)
            slot(G - 2, 0, prefetch=False)
            slot(G - 1, 1, prefetch=False)
            slot(G, 0, prefetch=False)
            sp.wait_ge(dma_out, 32 + 16 * G)

        @block.gpsimd
        def _(pool):
            nc.gpsimd.memset(one[:, :], 1.0)
            nc.gpsimd.memset(eps[:, :], LN_EPS)
            nc.gpsimd.memset(minus_half[:, :], -0.5).then_inc(pool_const, 1)
            nc.gpsimd.memset(ident[:, :], 0.0).then_inc(pool_ident, 1)
            pool.wait_ge(pool_ident, 1)
            nc.gpsimd.affine_select(out=ident[:, :], in_=ident[:, :], compare_op=ALU.not_equal, fill=1.0,
                                    base=0, pattern=[[-1, P]], channel_multiplier=1).then_inc(pool_ident, 1)

            def front_adj_sum(n, b):
                pool.wait_ge(act_exp_adj, n)
                nc.gpsimd.tensor_tensor(exp_adj[:, :, :], exp_adj[:, :, :], adj_sb[:, b], ALU.add) \
                    .then_inc(pool_adj_sum, 1)

            def front_extra(n, b, prob_before=0):
                pool.wait_ge(pool_adj_sum, n)
                pool.wait_ge(act_mask2, n)
                reuse(pool, dve_prob[1][0], prob_before)
                reuse(pool, dve_prob[1][1], prob_before)
                nc.gpsimd.tensor_tensor(extra[:, b], exp_adj[:, :, :], mask2[:, :, :], ALU.mult) \
                    .then_inc(pool_extra, 1)

            def norm_rstd(k, n):
                pool.wait_ge(dve_mv[k], n)
                nc.gpsimd.tensor_tensor(mv[:, k, :, 1], mv[:, k, :, 1], eps[:, :], ALU.add) \
                    .then_inc(pool_var[k], 1)
                pool.wait_ge(pool_var[k], n)
                nc.gpsimd.tensor_tensor(rstd[:, k], mv[:, k, :, 1], minus_half[:, :], ALU.pow) \
                    .then_inc(pool_rstd[k], 1)

            def columns(ap):
                return ap.unsqueeze(2).broadcast_to([P, NT, F])

            def x1_b3_sum(n, before=0):
                pool.wait_ge(dve_x[0], n)
                reuse(pool, dve_x2_pre, before)
                nc.gpsimd.tensor_tensor(x1_b3[:, :, :], x1[:, :, :],
                                        b3_row[:, :].unsqueeze(1).broadcast_to([P, NT, F]), ALU.add) \
                    .then_inc(pool_x1_b3, 1)

            def x2_bout_sum(n, b):
                pool.wait_ge(dve_x[1], n)
                nc.gpsimd.tensor_tensor(x2_bout[:, b], x2[:, :, :],
                                        bout_row[:, :].unsqueeze(1).broadcast_to([P, NT, F]), ALU.add) \
                    .then_inc(pool_x2_bout, 1)

            def tail_out(n):
                pool.wait_ge(act_gate_col, n)
                nc.gpsimd.tensor_tensor(x4_pre[:, :, :], qkv3[:, :, 2 * D:L3C], columns(gate_col[:, :]), ALU.mult) \
                    .then_inc(pool_gate_v, 1)
                pool.wait_ge(pool_gate_v, n)
                nc.gpsimd.tensor_tensor(x4_pre[:, :, :], x4_pre[:, :, :], x3[:, :, :], ALU.add) \
                    .then_inc(pool_x4_pre, 1)

            def tail_norm(n, b, stored):
                norm_rstd(3, n)
                pool.wait_ge(dma_out, stored)
                nc.gpsimd.tensor_tensor(y_sb[:, b], x4_pre[:, :, :], columns(mv[:, 3, :, 0]), ALU.subtract) \
                    .then_inc(pool_centred, 1)
                pool.wait_ge(pool_centred, n)
                pool.wait_ge(pool_rstd[3], n)
                nc.gpsimd.tensor_tensor(y_sb[:, b], y_sb[:, b], columns(rstd[:, 3]), ALU.mult) \
                    .then_inc(pool_y, 1)

            pool.wait_ge(pool_const, 1)
            front_adj_sum(1, 0)
            front_extra(1, 0)
            norm_rstd(0, 1)
            pool.wait_ge(dma_biases, 16 * BIAS_DMAS)
            x1_b3_sum(1)

            def slot(s, b, tail, front, ahead):
                c = Counts(pool, s)
                stored = 16 * s if isinstance(s, int) else pool.snap(16 * s)
                norm_rstd(1, c.att)
                if tail:
                    norm_rstd(2, c.tail)
                if front:
                    front_adj_sum(c.front, 1 - b)
                    norm_rstd(0, c.front)
                if tail:
                    tail_out(c.tail)
                x2_bout_sum(c.att, b)
                if tail:
                    tail_norm(c.tail, 1 - b, stored)
                if front:
                    front_extra(c.front, 1 - b, c.two[0])
                    x1_b3_sum(c.front, c.att)

            slots(pool, slot)
            norm_rstd(2, G)
            tail_out(G)
            tail_norm(G, 1, 16 * G)

        @block.scalar
        def _(act):
            def copy(dst, src, scale=1.0):
                return nc.scalar.activation(dst, src, ACT.Copy, scale=scale)

            def weight_hi(dst, src):
                return copy(dst, src).then_inc(act_w, 1)

            def front_mask(n, b, loaded, before=0):
                act.wait_ge(dma_graph[b], loaded)
                reuse(act, pe_mask2, before)
                copy(mask_row[:, :], mask_u8[:, b]).then_inc(act_mask_row, 1)

            def front_mask2(n, b, before=0, scores_before=0):
                act.wait_ge(pe_mask2, n)
                reuse(act, pool_extra, before)
                copy(mask2[:, :, :], halves(bank_f[:, 0])).then_inc(act_mask2, 1)
                for i in range(NT):
                    reuse(act, dve_scores[1][i], scores_before)
                nc.scalar.activation(minus_big[:, b], halves(bank_f[:, 0]), ACT.Copy, bias=-BIG, scale=BIG) \
                    .then_inc(act_minus_big, 1)

            def front_x(n):
                act.wait_ge(pe_xT, n)
                copy(fT[0][:, :, :], halves(bank_f[:, 1])).then_inc(act_xT, 1)

            def front_adj_t(n, b, before=0):
                act.wait_ge(pe_adjT, n)
                reuse(act, pe_adjk, before)
                copy(adjT[0][:, b], halves(bank_f[:, 2])).then_inc(act_adjT, 1)

            def front_from_adj(n, b, loaded, before=0):
                act.wait_ge(dma_graph[b], loaded)
                reuse(act, pool_extra, before)
                for t in range(NT):
                    last = nc.scalar.activation(adj_junk[:, t], adj_sb[:, b, t], ACT.Copy, accum_out=deg[:, t:t + 1])
                last.then_inc(act_deg, 1)
                nc.scalar.activation(exp_adj[:, :, :], adj_sb[:, b], ACT.Exp, scale=-1.0).then_inc(act_exp_adj, 1)

            def front_sup0(n):
                act.wait_ge(pe_proj0, n)
                copy(sup[0][:, :, :], bank_f[:, 0:2, F:2 * F]).then_inc(act_sup0, 1)

            def front_self(n):
                act.wait_ge(dve_sup0, n)
                copy(self_part[:, :, :], bank_f[:, 0:2, 0:F]).then_inc(act_self, 1)

            def hi(dst, bank, ready, n, done):
                act.wait_ge(ready, n)
                copy(dst, halves(bank)).then_inc(done, 1)

            def front_hidden(layer, n, bank, bias):
                act.wait_ge(pe_hid[layer], n)
                for h in range(FT):
                    last = nc.scalar.activation(hid[:, h], bank[:, h * N:(h + 1) * N], ACT.Relu,
                                                bias=bias[:, h:h + 1])
                last.then_inc(act_hid[layer], 1)
                act.wait_ge(act_hid[layer], n)
                copy(hidT[0][:, :, :], hid[:, :, :]).then_inc(act_hid_hi[layer], 1)

            def values(n):
                act.wait_ge(pe_v, n)
                copy(v_sb[:, :, :], bank_d[:, :, :], scale=MIX).then_inc(act_v, 1)

            def qk(p, c):
                act.wait_ge(pe_qk[p % 2], c.pair(p))
                copy(qT[0][:, p % 2], bank_q[:, 0:N])
                copy(kTz[0][0:D, p % 2, 0], bank_q[0:D, N:2 * N])
                copy(kTz[0][D:P, p % 2, 1], bank_q[D:P, N:2 * N]).then_inc(act_qk[p % 2], 1)

            def exps(p, i, c):
                act.wait_ge(dve_scores[p % 2][i], c.pair(p))
                for h in range(2):
                    last = nc.scalar.activation(prob[:, p % 2, i, h], prob[:, p % 2, i, h], ACT.Exp,
                                                bias=shift[:, p % 2, h, i:i + 1], scale=-1.0,
                                                accum_out=psum_exp[:, p % 2, h, i:i + 1])
                last.then_inc(act_exp[p % 2][i], 1)

            def probs_t(p, h, c):
                act.wait_ge(pe_probT[p % 2][h], c.pair(p))
                if h == 0:
                    reuse(act, pe_pv[p % 2], c.pair(p, 1))
                copy(probT[:, p % 2, h], halves(bank_t[:, :])).then_inc(act_probT[p % 2][h], 1)

            def out_t(p, c):
                act.wait_ge(pe_pv[p % 2], c.pair(p))
                copy(oT[0][:, p], bank_o[:, 0:N]).then_inc(act_oT[p % 2], 1)

            def tail_qkv(n):
                act.wait_ge(pe_proj3, n)
                copy(qkv3[:, :, :], bank_d[:, :, 0:L3C]).then_inc(act_qkv3, 1)

            def tail_exp(n):
                act.wait_ge(dve_gate_shift, n)
                nc.scalar.activation(gate_exp[:, :], bank_o[0:1, 0:N], ACT.Exp, bias=gate_shift[:, :],
                                     accum_out=gate_sum[:, :]).then_inc(act_gate_exp, 1)

            def tail_col(n):
                act.wait_ge(pe_gate_col, n)
                copy(gate_col[:, :], bank_o[:, 0:NT]).then_inc(act_gate_col, 1)

            front_mask(1, 0, 48)
            front_x(1)
            front_adj_t(1, 0)
            act.wait_ge(pe_w, 1)
            weight_hi(w0[0][:, :, :], bank_d[:, :, :])
            front_mask2(1, 0)
            front_from_adj(1, 0, 48)
            act.wait_ge(dma_w123, 16 * 3)
            weight_hi(w123[0][:, 0], w123_raw[:, 0])
            front_sup0(1)
            front_self(1)
            for i in (1, 2):
                weight_hi(w123[0][:, i], w123_raw[:, i])
            act.wait_ge(pe_w, 2)
            copy(w3[0][:, 0], bank_q[:, 0:L3C])
            weight_hi(w3[0][:, 1], bank_t[:, 0:L3C])
            hi(fT[0][:, :, :], bank_f[:, 0], pe_x1T, 1, act_x1T)
            act.wait_ge(dma_wqkv, 16)
            for k in range(FT):
                weight_hi(wqkv[0][:, k].rearrange("p i (h d) -> p i h d", d=D),
                          wqkv_raw[:, k].rearrange("p (h i d) -> p i h d", i=3, d=D))
            hi(sup[0][:, :, :], bank_f[:, 1], pe_sup[0], 1, act_sup[0])
            act.wait_ge(dma_wout, 16)
            weight_hi(wout[0][:, :, :], wout_raw[:, :, :])
            act.wait_ge(dma_biases, 16 * BIAS_DMAS)
            front_hidden(0, 1, bank_f[:, 2], b1_col)
            hi(sup[0][:, :, :], bank_f[:, 0], pe_sup[1], 1, act_sup[1])
            front_hidden(1, 1, bank_f[:, 1], b2_col)
            hi(sup[0][:, :, :], bank_f[:, 2], pe_sup[2], 1, act_sup[2])

            front_mask(2, 1, 48, 1)
            front_mask2(2, 1, 1, 0)
            front_x(2)

            def slot(s, b, tail, front, ahead):
                c = Counts(act, s)
                if front:
                    loaded = loads_done(act, s, b, 1)
                if ahead:
                    loaded_ahead = loads_done(act, s, b, 2)
                if ahead:
                    front_mask(c.ahead, b, loaded_ahead, c.front)
                hi(x2T[0][:, :, :], bank_q[:, :], pe_x2T, c.att, act_x2T)
                if front:
                    front_from_adj(c.front, 1 - b, loaded, c.att)
                values(c.att)
                if tail:
                    hi(x3T[0][:, :, :], bank_o[:, :], pe_x3T, c.tail, act_x3T)
                qk(0, c)
                if tail:
                    tail_qkv(c.tail)
                if front:
                    front_sup0(c.front)
                    front_adj_t(c.front, 1 - b, c.tail)
                    front_self(c.front)
                qk(1, c)
                exps(0, 0, c)
                qk(2, c)
                if tail:
                    tail_exp(c.tail)
                exps(0, 1, c)
                exps(1, 0, c)
                if front:
                    hi(fT[0][:, :, :], bank_f[:, 0], pe_x1T, c.front, act_x1T)
                exps(1, 1, c)
                probs_t(0, 0, c)
                if front:
                    hi(sup[0][:, :, :], bank_f[:, 1], pe_sup[0], c.front, act_sup[0])
                probs_t(0, 1, c)
                qk(3, c)
                if front:
                    front_hidden(0, c.front, bank_f[:, 2], b1_col)
                probs_t(1, 0, c)
                if tail:
                    tail_col(c.tail)
                exps(2, 0, c)
                if front:
                    hi(sup[0][:, :, :], bank_f[:, 0], pe_sup[1], c.front, act_sup[1])
                exps(2, 1, c)
                probs_t(1, 1, c)
                out_t(0, c)
                exps(3, 0, c)
                if front:
                    front_hidden(1, c.front, bank_f[:, 1], b2_col)
                out_t(1, c)
                exps(3, 1, c)
                probs_t(2, 0, c)
                if front:
                    hi(sup[0][:, :, :], bank_f[:, 2], pe_sup[2], c.front, act_sup[2])
                probs_t(2, 1, c)
                probs_t(3, 0, c)
                out_t(2, c)
                probs_t(3, 1, c)
                if ahead:
                    front_mask2(c.ahead, b, c.front, c.two[2])
                    front_x(c.ahead)
                out_t(3, c)

            slots(act, slot)
            hi(x3T[0][:, :, :], bank_o[:, :], pe_x3T, G, act_x3T)
            tail_qkv(G)
            tail_exp(G)
            tail_col(G)

        @block.vector
        def _(dve):
            V = nc.vector

            def f32(ap):
                return ap.bitcast(F32)

            def lo(dst, src, hi_part):
                return V.tensor_tensor(dst, src, f32(hi_part), ALU.subtract)

            for part in range(2):
                V.memset(f32(kTz[part][D:P, :, 0]), 0.0)
                V.memset(f32(kTz[part][0:D, :, 1]), 0.0).then_inc(dve_zero, 1)
            def weight_lo(dst, src, hi_part, number, last=True):
                dve.wait_ge(act_w, number)
                step = lo(dst, src, hi_part)
                if last:
                    step.then_inc(dve_w, 1)

            def wqkv_lo(k):
                for i in range(3):
                    weight_lo(wqkv[1][:, k, i].rearrange("p (h d) -> p h d", d=D),
                              wqkv_raw[:, k].rearrange("p (h i d) -> p i h d", i=3, d=D)[:, i],
                              wqkv[0][:, k, i].rearrange("p (h d) -> p h d", d=D), W_QKV + k, last=i == 2)

            def split(parts, src, ready, n, done):
                dve.wait_ge(ready, n)
                lo(parts[1], src, parts[0]).then_inc(done, 1)

            def fixed_wait():
                dve.wait_ge(dve_zero, 2)

            def norm_stats(k, src, ready, n):
                dve.wait_ge(ready, n)
                for t in range(NT):
                    last = V.bn_stats(out=bn[:, k, t], in_=src[:, t])
                last.then_inc(dve_bn[k], 1)
                fixed_wait()
                dve.wait_ge(dve_bn[k], n)
                for t in range(NT):
                    last = V.bn_aggr(out=mv[:, k, t], in_=bn[:, k, t])
                last.then_inc(dve_mv[k], 1)

            def norm_apply(k, src, dst, n, done):
                dve.wait_ge(pool_rstd[k], n)
                for t in range(NT):
                    last = V.tensor_scalar(dst[:, t], src[:, t], mv[:, k, t, 0:1], rstd[:, k, t:t + 1],
                                           ALU.subtract, ALU.mult)
                last.then_inc(done, 1)

            def front_x(n):
                split([a[:, :, :] for a in fT], halves(bank_f[:, 1]), act_xT, n, dve_xT)

            def front_adj_t(n, b):
                split([a[:, b] for a in adjT], halves(bank_f[:, 2]), act_adjT, n, dve_adjT)

            def front_degrees(n):
                dve.wait_ge(act_deg, n)
                V.tensor_scalar(rdeg[:, :], deg[:, :], DEG_EPS, None, ALU.max).then_inc(dve_deg, 1)
                dve.wait_ge(dve_deg, n)
                V.reciprocal(rdeg[:, :], rdeg[:, :]).then_inc(dve_rdeg, 1)

            def front_sup0(n):
                split([a[:, :, :] for a in sup], bank_f[:, 0:2, F:2 * F], act_sup0, n, dve_sup0)

            def front_agg(n, b):
                dve.wait_ge(pe_agg, n)
                dve.wait_ge(act_self, n)
                dve.wait_ge(dve_rdeg, n)
                for t in range(NT):
                    last = V.scalar_tensor_tensor(out=x1_pre[:, t], in0=bank_f[:, 2, t * F:(t + 1) * F],
                                                  scalar=rdeg[:, t:t + 1], in1=self_part[:, t],
                                                  op0=ALU.mult, op1=ALU.add)
                last.then_inc(dve_agg, 1)
                dve.wait_ge(dve_agg, n)
                V.scalar_tensor_tensor(out=x1_pre[:, :, :], in0=x1_pre[:, :, :], scalar=0.0, in1=x_sb[:, b],
                                       op0=ALU.max, op1=ALU.add).then_inc(dve_x1_pre, 1)
                norm_stats(0, x1_pre, dve_x1_pre, n)

            def front_hidden(layer, n):
                split([a[:, :, :] for a in hidT], hid[:, :, :], act_hid_hi[layer], n, dve_hid[layer])

            def front_out(n):
                dve.wait_ge(pe_gcn, n)
                dve.wait_ge(pool_x1_b3, n)
                V.tensor_tensor(x2_pre[:, :, :], halves(bank_q[:, :]), x1_b3[:, :, :], ALU.add) \
                    .then_inc(dve_x2_pre, 1)
                norm_stats(1, x2_pre, dve_x2_pre, n)

            def qk(p, c):
                if p < 2:
                    reuse(dve, pe_probT[p % 2][1], c.pair(p, 1))
                if p == 0:
                    dve.wait_ge(act_minus_big, c.att)
                dve.wait_ge(act_qk[p % 2], c.pair(p))
                lo(qT[1][:, p % 2], bank_q[:, 0:N], qT[0][:, p % 2])
                lo(kTz[1][0:D, p % 2, 0], bank_q[0:D, N:2 * N], kTz[0][0:D, p % 2, 0])
                lo(kTz[1][D:P, p % 2, 1], bank_q[D:P, N:2 * N], kTz[0][D:P, p % 2, 1]).then_inc(dve_qk[p % 2], 1)

            def scores(p, i, c, b, first):
                fixed_wait()
                if first and p > 1:
                    dve.wait_ge(pe_probT[p % 2][1], c.pair(p, 1))
                dve.wait_ge(pe_scores[p % 2][i], c.pair(p))
                for h in range(2):
                    last = V.tensor_tensor_reduce(
                        out=prob[:, p % 2, i, h], in0=bank_d[:, i, h * N:(h + 1) * N],
                        in1=minus_big[:, b, i], scale=-QK_SCALE, scalar=3.0e38, op0=ALU.add, op1=ALU.min,
                        accum_out=shift[:, p % 2, h, i:i + 1])
                last.then_inc(dve_scores[p % 2][i], 1)

            def probs(p, h, c, b, first):
                if first:
                    for i in range(NT):
                        dve.wait_ge(act_exp[p % 2][i], c.pair(p))
                    V.reciprocal(rsum[:, p % 2], psum_exp[:, p % 2]).then_inc(dve_rsum[p % 2], 1)
                    dve.wait_ge(dve_rsum[p % 2], c.pair(p))
                for i in range(NT):
                    last = V.scalar_tensor_tensor(out=prob[:, p % 2, i, h], in0=prob[:, p % 2, i, h],
                                                  scalar=rsum[:, p % 2, h, i:i + 1], in1=extra[:, b, i],
                                                  op0=ALU.mult, op1=ALU.add)
                last.then_inc(dve_prob[p % 2][h], 1)

            def out_t(p, c):
                dve.wait_ge(act_oT[p % 2], c.pair(p))
                lo(oT[1][:, p], bank_o[:, 0:N], oT[0][:, p]).then_inc(dve_oT[p % 2], 1)

            def attention_out(n, b):
                dve.wait_ge(pe_y, n)
                dve.wait_ge(pool_x2_bout, n)
                V.tensor_tensor(x3_pre[:, :, :], halves(bank_t[:, :]), x2_bout[:, b], ALU.add) \
                    .then_inc(dve_x3_pre, 1)
                norm_stats(2, x3_pre, dve_x3_pre, n)

            def tail_k(n):
                dve.wait_ge(act_qkv3, n)
                V.tensor_copy(k3[:, :, 0], qkv3[:, :, D:2 * D]).then_inc(dve_k3_hi, 1)
                dve.wait_ge(dve_k3_hi, n)
                lo(k3[:, :, 1], qkv3[:, :, D:2 * D], k3[:, :, 0]).then_inc(dve_k3, 1)

            def tail_gate(n):
                dve.wait_ge(pe_adjk, n)
                for t in range(NT):
                    last = V.tensor_tensor_reduce(
                        out=gate_junk[:, t], in0=bank_o[:, t * P:(t + 1) * P].rearrange("p (a d) -> p a d", a=2),
                        in1=qkv3[:, t, 0:D].unsqueeze(1).broadcast_to([P, 2, D]), scale=QK_SCALE, scalar=0.0,
                        op0=ALU.mult, op1=ALU.add, accum_out=gate[:, t:t + 1])
                last.then_inc(dve_gate, 1)

            def tail_max(n):
                dve.wait_ge(pe_gate_row, n)
                V.tensor_reduce(gate_max[:, :], bank_o[0:1, 0:N], AX.X, ALU.max).then_inc(dve_gate_max, 1)
                dve.wait_ge(dve_gate_max, n)
                V.tensor_scalar(gate_shift[:, :], gate_max[:, :], -1.0, None, ALU.mult).then_inc(dve_gate_shift, 1)

            def tail_prob(n):
                dve.wait_ge(act_gate_exp, n)
                V.reciprocal(gate_rsum[:, :], gate_sum[:, :]).then_inc(dve_gate_rsum, 1)
                dve.wait_ge(dve_gate_rsum, n)
                V.tensor_scalar(gate_prob[:, :], gate_exp[:, :], gate_rsum[:, :], None, ALU.mult) \
                    .then_inc(dve_gate_prob, 1)

            front_x(1)
            front_adj_t(1, 0)
            weight_lo(w0[1][:, :, :], bank_d[:, :, :], w0[0][:, :, :], W0)
            front_degrees(1)
            weight_lo(w123[1][:, 0], w123_raw[:, 0], w123[0][:, 0], W1)
            front_sup0(1)
            front_agg(1, 0)
            weight_lo(w123[1][:, 1], w123_raw[:, 1], w123[0][:, 1], W1 + 1)
            norm_apply(0, x1_pre, x1, 1, dve_x[0])
            weight_lo(w123[1][:, 2], w123_raw[:, 2], w123[0][:, 2], W3TH)
            weight_lo(w3[1][:, 0], bank_q[:, 0:L3C], w3[0][:, 0], W_LAST, last=False)
            weight_lo(w3[1][:, 1], bank_t[:, 0:L3C], w3[0][:, 1], W_LAST)
            split([a[:, :, :] for a in fT], halves(bank_f[:, 0]), act_x1T, 1, dve_x1T)
            wqkv_lo(0)
            split([a[:, :, :] for a in sup], halves(bank_f[:, 1]), act_sup[0], 1, dve_sup[0])
            wqkv_lo(1)
            front_hidden(0, 1)
            weight_lo(wout[1][:, :, :], wout_raw[:, :, :], wout[0][:, :, :], W_OUT)
            split([a[:, :, :] for a in sup], halves(bank_f[:, 0]), act_sup[1], 1, dve_sup[1])
            front_hidden(1, 1)
            split([a[:, :, :] for a in sup], halves(bank_f[:, 2]), act_sup[2], 1, dve_sup[2])

            front_out(1)
            norm_apply(1, x2_pre, x2, 1, dve_x[1])
            split([a[:, :, :] for a in x2T], halves(bank_q[:, :]), act_x2T, 1, dve_x2T)
            front_x(2)
            front_degrees(2)

            def slot(s, b, tail, front, ahead):
                c = Counts(dve, s)
                qk(0, c)
                if tail:
                    tail_k(c.tail)
                if front:
                    front_sup0(c.front)
                    front_adj_t(c.front, 1 - b)
                if tail:
                    tail_gate(c.tail)
                scores(0, 0, c, b, first=True)
                scores(0, 1, c, b, first=False)
                if tail:
                    tail_max(c.tail)
                qk(1, c)
                if front:
                    front_agg(c.front, 1 - b)
                qk(2, c)
                scores(1, 0, c, b, first=True)
                if front:
                    norm_apply(0, x1_pre, x1, c.front, dve_x[0])
                probs(0, 0, c, b, first=True)
                scores(1, 1, c, b, first=False)
                if front:
                    split([a[:, :, :] for a in fT], halves(bank_f[:, 0]), act_x1T, c.front, dve_x1T)
                probs(0, 1, c, b, first=False)
                probs(1, 0, c, b, first=True)
                if front:
                    split([a[:, :, :] for a in sup], halves(bank_f[:, 1]), act_sup[0], c.front, dve_sup[0])
                scores(2, 0, c, b, first=True)
                if tail:
                    tail_prob(c.tail)
                qk(3, c)
                if front:
                    front_hidden(0, c.front)
                probs(1, 1, c, b, first=False)
                scores(2, 1, c, b, first=False)
                if front:
                    split([a[:, :, :] for a in sup], halves(bank_f[:, 0]), act_sup[1], c.front, dve_sup[1])
                scores(3, 0, c, b, first=True)
                if tail:
                    norm_stats(3, x4_pre, pool_x4_pre, c.tail)
                out_t(0, c)
                probs(2, 0, c, b, first=True)
                scores(3, 1, c, b, first=False)
                if front:
                    front_hidden(1, c.front)
                probs(2, 1, c, b, first=False)
                probs(3, 0, c, b, first=True)
                if front:
                    split([a[:, :, :] for a in sup], halves(bank_f[:, 2]), act_sup[2], c.front, dve_sup[2])
                out_t(1, c)
                probs(3, 1, c, b, first=False)
                out_t(2, c)
                if front:
                    front_out(c.front)
                out_t(3, c)
                if front:
                    norm_apply(1, x2_pre, x2, c.front, dve_x[1])
                attention_out(c.att, b)
                if front:
                    split([a[:, :, :] for a in x2T], halves(bank_q[:, :]), act_x2T, c.front, dve_x2T)
                if ahead:
                    front_x(c.ahead)
                norm_apply(2, x3_pre, x3, c.att, dve_x[2])
                if ahead:
                    front_degrees(c.ahead)
                split([a[:, :, :] for a in x3T], halves(bank_o[:, :]), act_x3T, c.att, dve_x3T)

            slots(dve, slot)
            tail_k(G)
            tail_gate(G)
            tail_max(G)
            tail_prob(G)
            norm_stats(3, x4_pre, pool_x4_pre, G)

        @block.tensor
        def _(pe):
            mm = nc.tensor.matmul
            HI, LO = 0, 1
            ALL = ((0, 0), (0, 1), (1, 0))
            LEFT_LATE = (((0, 0), (0, 1)), ((1, 0),))
            RIGHT_LATE = (((0, 0), (1, 0)), ((0, 1),))
            BOTH_LATE = (((0, 0),), ((0, 1), (1, 0)))

            def product(dst, terms, passes=ALL, opens=True, closes=True):
                steps = [(left[a], right[b]) for left, right in terms for a, b in passes]
                for n, (left, right) in enumerate(steps):
                    last = mm(dst, left, right, start=opens and n == 0, stop=closes and n == len(steps) - 1)
                return last

            def cut(parts, *index):
                return [a[index] for a in parts]

            A = slice(None)

            def block_of(i, size=P):
                return slice(i * size, (i + 1) * size)

            def transpose_tiles(bank, src):
                for r in range(2):
                    for t in range(2):
                        last = nc.tensor.transpose(bank[:, r * N + t * P:r * N + (t + 1) * P],
                                                   src[:, t, block_of(r)], ident[:, :])
                return last

            x1T_ready = (act_x1T, dve_x1T)
            hidT_ready = [(act_hid_hi[i], dve_hid[i]) for i in range(2)]

            def mask_product(n, before=0):
                pe.wait_ge(act_mask_row, n)
                reuse(pe, dve_sup[1], before)
                for t in range(NT):
                    last = mm(bank_f[:, 0, t * N:(t + 1) * N], mask_row[:, block_of(t)], mask_row[:, :],
                              start=True, stop=True)
                last.then_inc(pe_mask2, 1)

            def x_transpose(n, b, loaded, before=0):
                pe.wait_ge(dma_graph[b], loaded)
                reuse(pe, act_hid[1], before)
                transpose_tiles(bank_f[:, 1], x_sb[:, b]).then_inc(pe_xT, 1)

            def adj_transpose(n, b, loaded, before=0):
                pe.wait_ge(dma_graph[b], loaded)
                reuse(pe, dve_sup[2], before)
                transpose_tiles(bank_f[:, 2], adj_sb[:, b]).then_inc(pe_adjT, 1)

            def front_project(n, part):
                if part == HI:
                    pe.wait_ge(act_xT, n)
                    pe.wait_ge(act_minus_big, n)
                else:
                    pe.wait_ge(dve_xT, n)
                for t in range(NT):
                    terms = [(cut(fT, A, k, block_of(t)), cut(w0, A, k)) for k in range(FT)]
                    if t == 0:
                        product(bank_f[:, t, :], terms, LEFT_LATE[part], opens=part == HI, closes=part == LO)
                    elif part == LO:
                        product(bank_f[:, t, :], terms).then_inc(pe_proj0, 1)

            def adj_times_support(bank, b, part):
                for t in range(NT):
                    last = product(bank[:, t * F:(t + 1) * F],
                                   [(cut(adjT, A, b, k, block_of(t)), cut(sup, A, k)) for k in range(NT)],
                                   RIGHT_LATE[part], opens=part == HI and t == 0,
                                   closes=part == LO and t == NT - 1)
                return last

            def front_aggregate(n, b, part):
                if part == HI:
                    pe.wait_ge(act_sup0, n)
                    pe.wait_ge(dve_adjT, n)
                    adj_times_support(bank_f[:, 2], b, HI)
                else:
                    pe.wait_ge(dve_sup0, n)
                    adj_times_support(bank_f[:, 2], b, LO).then_inc(pe_agg, 1)

            def front_x1_transpose(n):
                pe.wait_ge(dve_x[0], n)
                transpose_tiles(bank_f[:, 0], x1).then_inc(pe_x1T, 1)

            def front_support(layer, n, bank, src, ready, part):
                pe.wait_ge(ready[part], n)
                for t in range(NT):
                    last = product(bank[:, t * F:(t + 1) * F],
                                   [(cut(src, A, k, block_of(t)), cut(w123, A, layer, k)) for k in range(FT)],
                                   LEFT_LATE[part], opens=part == HI and t == 0,
                                   closes=part == LO and t == NT - 1)
                if part == LO:
                    last.then_inc(pe_sup[layer], 1)

            def front_hidden(layer, n, bank, b, part):
                pe.wait_ge((act_sup, dve_sup)[part][layer], n)
                for h in range(FT):
                    last = product(bank[:, h * N:(h + 1) * N],
                                   [(cut(sup, A, k, block_of(h)), cut(adjT, A, b, k)) for k in range(NT)],
                                   LEFT_LATE[part], opens=part == HI and h == 0,
                                   closes=part == LO and h == FT - 1)
                if part == LO:
                    last.then_inc(pe_hid[layer], 1)

            def front_out(n, b, part, before=0):
                if part == HI:
                    pe.wait_ge(act_sup[2], n)
                    reuse(pe, dve_qk[1], before)
                    adj_times_support(bank_q[:, :], b, HI)
                else:
                    pe.wait_ge(dve_sup[2], n)
                    adj_times_support(bank_q[:, :], b, LO).then_inc(pe_gcn, 1)

            def x2_transpose(n):
                pe.wait_ge(dve_x[1], n)
                transpose_tiles(bank_q[:, :], x2).then_inc(pe_x2T, 1)

            def values(n, part):
                pe.wait_ge((act_x2T, dve_x2T)[part], n)
                for t in range(NT):
                    last = product(bank_d[:, t, :],
                                   [(cut(x2T, A, k, block_of(t)), cut(wqkv, A, k, 2)) for k in range(FT)],
                                   LEFT_LATE[part], opens=part == HI, closes=part == LO)
                if part == LO:
                    last.then_inc(pe_v, 1)

            def qk(p, c):
                if p:
                    pe.wait_ge(dve_qk[(p - 1) % 2], c.pair(p - 1))
                else:
                    pe.wait_ge(dve_x2T, c.att)
                for i in range(2):
                    last = product(bank_q[:, i * N:(i + 1) * N],
                                   [(cut(wqkv, A, k, i, block_of(p)), cut(x2T, A, k)) for k in range(FT)])
                last.then_inc(pe_qk[p % 2], 1)

            def scores(p, i, c, part, tail, first):
                if first:
                    pe.wait_ge((act_qk, dve_qk)[part][p % 2], c.pair(p))
                if part == HI:
                    if p:
                        pe.wait_ge(dve_scores[(p - 1) % 2][i], c.pair(p - 1))
                    elif first and tail:
                        pe.wait_ge(act_qkv3, c.tail)
                last = product(bank_d[:, i, :],
                               [(cut(qT, A, p % 2, block_of(i)),
                                 [a[:, p % 2].rearrange("p h n -> p (h n)") for a in kTz])],
                               BOTH_LATE[part], opens=part == HI, closes=part == LO)
                if part == LO:
                    last.then_inc(pe_scores[p % 2][i], 1)

            def probs_t(p, h, c, tail):
                pe.wait_ge(dve_prob[p % 2][h], c.pair(p))
                if h:
                    pe.wait_ge(act_probT[p % 2][0], c.pair(p))
                elif p:
                    pe.wait_ge(act_probT[(p - 1) % 2][1], c.pair(p - 1))
                elif tail:
                    pe.wait_ge(dve_x3_pre, c.tail)
                transpose_tiles(bank_t[:, :], prob[:, p % 2, :, h]).then_inc(pe_probT[p % 2][h], 1)

            def attend(p, c, tail):
                pe.wait_ge(act_probT[p % 2][1], c.pair(p))
                if p:
                    pe.wait_ge(dve_oT[(p - 1) % 2], c.pair(p - 1))
                else:
                    pe.wait_ge(act_v, c.att)
                    if tail:
                        pe.wait_ge(act_gate_col, c.tail)
                for k in range(NT):
                    for h in range(2):
                        last = mm(bank_o[h * D:(h + 1) * D, 0:N], v_sb[:, k, (2 * p + h) * D:(2 * p + h + 1) * D],
                                  probT[:, p % 2, h, k], start=k == 0, stop=k == NT - 1)
                last.then_inc(pe_pv[p % 2], 1)

            def project_out(pairs, part):
                if part == HI:
                    pe.wait_ge(dve_oT[0], pairs)
                    pe.wait_ge(act_probT[1][1], pairs)
                else:
                    pe.wait_ge(dve_oT[1], pairs)
                for t in range(NT):
                    last = product(bank_t[:, t * F:(t + 1) * F],
                                   [(cut(oT, A, p, block_of(t)), cut(wout, A, p))
                                    for p in ((0, 1, 2), (3,))[part]],
                                   opens=part == HI and t == 0,
                                   closes=part == LO and t == NT - 1)
                if part == LO:
                    last.then_inc(pe_y, 1)

            def tail_transpose(n):
                pe.wait_ge(dve_x[2], n)
                transpose_tiles(bank_o[:, :], x3).then_inc(pe_x3T, 1)

            def tail_project(n, part, after_v=0):
                pe.wait_ge((act_x3T, dve_x3T)[part], n)
                if part == HI:
                    reuse(pe, act_v, after_v)
                for t in range(NT):
                    last = product(bank_d[:, t, 0:L3C],
                                   [(cut(x3T, A, k, block_of(t)), cut(w3, A, k)) for k in range(FT)],
                                   LEFT_LATE[part], opens=part == HI, closes=part == LO)
                if part == LO:
                    last.then_inc(pe_proj3, 1)

            def tail_adj_k(n, b):
                pe.wait_ge(dve_k3, n)
                for t in range(NT):
                    at = t * P
                    for k in range(NT):
                        mm(bank_o[:, at:at + 2 * D], adjT[0][:, b, k, block_of(t)],
                           k3[:, k].rearrange("p a d -> p (a d)"), start=k == 0, stop=False)
                    for k in range(NT):
                        last = mm(bank_o[:, at:at + D], adjT[1][:, b, k, block_of(t)], k3[:, k, 0],
                                  start=False, stop=k == NT - 1)
                last.then_inc(pe_adjk, 1)

            def tail_gate_row(n):
                pe.wait_ge(dve_gate, n)
                for t in range(NT):
                    last = nc.tensor.transpose(bank_o[0:1, t * P:(t + 1) * P], gate[:, t:t + 1], ident[:, :])
                last.then_inc(pe_gate_row, 1)

            def tail_gate_col(n):
                pe.wait_ge(dve_gate_prob, n)
                for t in range(NT):
                    last = mm(bank_o[:, t:t + 1], gate_prob[:, block_of(t)], one[:, :], start=True, stop=True)
                last.then_inc(pe_gate_col, 1)

            pe.wait_ge(pool_ident, 2)
            x_transpose(1, 0, 48)
            adj_transpose(1, 0, 48)
            pe.wait_ge(dma_w0, 16)
            for k in range(FT):
                for o in range(2):
                    for half in range(FT):
                        last = nc.tensor.transpose(bank_d[:, k, o * F + half * P:o * F + (half + 1) * P],
                                                   w0_raw[:, half, o * F + k * P:o * F + (k + 1) * P],
                                                   ident[:, :])
            last.then_inc(pe_w, 1)
            mask_product(1)
            pe.wait_ge(dve_w, W0)
            for part in (HI, LO):
                front_project(1, part)
            for part in (HI, LO):
                front_aggregate(1, 0, part)
            pe.wait_ge(dma_w3, 16 * 2)
            for k, bank in enumerate((bank_q, bank_t)):
                nc.tensor.transpose(bank[:, 0:P], wqk3_raw[:, block_of(k)], ident[:, :])
                for o in range(FT):
                    last = nc.tensor.transpose(bank[:, P + o * P:P + (o + 1) * P],
                                               wv3_raw[:, o, block_of(k)], ident[:, :])
            last.then_inc(pe_w, 1)
            front_x1_transpose(1)
            pe.wait_ge(dve_w, W1)
            for part in (HI, LO):
                front_support(0, 1, bank_f[:, 1], fT, x1T_ready, part)
            for part in (HI, LO):
                front_hidden(0, 1, bank_f[:, 2], 0, part)
            pe.wait_ge(dve_w, W1 + 1)
            for part in (HI, LO):
                front_support(1, 1, bank_f[:, 0], hidT, hidT_ready[0], part)
            for part in (HI, LO):
                front_hidden(1, 1, bank_f[:, 1], 0, part)
            pe.wait_ge(dve_w, W3TH)
            for part in (HI, LO):
                front_support(2, 1, bank_f[:, 2], hidT, hidT_ready[1], part)
            pe.wait_ge(dve_w, W_OUT)
            pe.wait_ge(dve_zero, 2)

            mask_product(2, 1)
            x_transpose(2, 1, 48, 1)
            front_out(1, 0, HI, 0)
            front_out(1, 0, LO)
            adj_transpose(2, 1, 48, 1)
            x2_transpose(1)

            def slot(s, b, tail, front, ahead):
                c = Counts(pe, s)
                if ahead:
                    loaded_ahead = loads_done(pe, s, b, 2)
                if front:
                    front_project(c.front, HI)
                values(c.att, HI)
                values(c.att, LO)
                if tail:
                    tail_transpose(c.tail)
                qk(0, c)
                if tail:
                    tail_project(c.tail, HI, c.att)
                    tail_project(c.tail, LO)
                if front:
                    front_project(c.front, LO)
                if tail:
                    tail_adj_k(c.tail, 1 - b)
                scores(0, 1, c, HI, tail, first=True)
                scores(0, 0, c, HI, tail, first=False)
                scores(0, 1, c, LO, tail, first=True)
                scores(0, 0, c, LO, tail, first=False)
                qk(1, c)
                if tail:
                    tail_gate_row(c.tail)
                if front:
                    front_aggregate(c.front, 1 - b, HI)
                    front_aggregate(c.front, 1 - b, LO)
                qk(2, c)
                scores(1, 1, c, HI, tail, first=True)
                scores(1, 0, c, HI, tail, first=False)
                scores(1, 0, c, LO, tail, first=True)
                scores(1, 1, c, LO, tail, first=False)
                qk(3, c)
                if front:
                    front_x1_transpose(c.front)
                scores(2, 0, c, HI, tail, first=True)
                probs_t(0, 0, c, tail)
                if front:
                    front_support(0, c.front, bank_f[:, 1], fT, x1T_ready, HI)
                    front_support(0, c.front, bank_f[:, 1], fT, x1T_ready, LO)
                scores(2, 0, c, LO, tail, first=True)
                probs_t(0, 1, c, tail)
                if front:
                    front_hidden(0, c.front, bank_f[:, 2], 1 - b, HI)
                    front_hidden(0, c.front, bank_f[:, 2], 1 - b, LO)
                scores(2, 1, c, HI, tail, first=False)
                probs_t(1, 0, c, tail)
                scores(3, 0, c, HI, tail, first=True)
                if tail:
                    tail_gate_col(c.tail)
                scores(2, 1, c, LO, tail, first=False)
                if front:
                    front_support(1, c.front, bank_f[:, 0], hidT, hidT_ready[0], HI)
                    front_support(1, c.front, bank_f[:, 0], hidT, hidT_ready[0], LO)
                scores(3, 0, c, LO, tail, first=True)
                probs_t(1, 1, c, tail)
                attend(0, c, tail)
                if front:
                    front_hidden(1, c.front, bank_f[:, 1], 1 - b, HI)
                    front_hidden(1, c.front, bank_f[:, 1], 1 - b, LO)
                scores(3, 1, c, HI, tail, first=False)
                scores(3, 1, c, LO, tail, first=False)
                if ahead:
                    mask_product(c.ahead, c.front)
                attend(1, c, tail)
                probs_t(2, 0, c, tail)
                if front:
                    front_support(2, c.front, bank_f[:, 2], hidT, hidT_ready[1], HI)
                    front_support(2, c.front, bank_f[:, 2], hidT, hidT_ready[1], LO)
                if ahead:
                    x_transpose(c.ahead, b, loaded_ahead, c.front)
                probs_t(2, 1, c, tail)
                if front:
                    front_out(c.front, 1 - b, HI, c.two[2])
                probs_t(3, 0, c, tail)
                attend(2, c, tail)
                probs_t(3, 1, c, tail)
                if front:
                    front_out(c.front, 1 - b, LO)
                if ahead:
                    adj_transpose(c.ahead, b, loaded_ahead, c.front)
                attend(3, c, tail)
                project_out(c.two[2], HI)
                project_out(c.two[2], LO)
                if front:
                    x2_transpose(c.front)

            slots(pe, slot)
            tail_transpose(G)
            tail_project(G, HI, 0)
            tail_project(G, LO)
            tail_adj_k(G, 1)
            tail_gate_row(G)
            tail_gate_col(G)


_INS = ["x", "adj", "nodemask", "L0_gnn_W", "L1_gnn_W1", "L1_gnn_b1", "L1_gnn_W2", "L1_gnn_b2", "L1_gnn_W3",
        "L1_gnn_b3", "L2_gnn_W_qkv", "L2_gnn_W_out", "L2_gnn_b_out", "L3_gnn_W_qk", "L3_gnn_W_v"]


def kernel(**inputs):
    import numpy as _np
    import concourse.bacc as _bacc
    from concourse import mybir as _mybir
    from concourse.bass_utils import run_bass_kernel_spmd as _run

    nc = _bacc.Bacc("TRN2", target_bir_lowering=False, num_devices=1)
    arrays, args = {}, []
    for name in _INS:
        a = _np.ascontiguousarray(inputs[name])
        arrays[f"in_{name}"] = a
        args.append(nc.dram_tensor(f"in_{name}", a.shape, _mybir.dt.from_np(a.dtype), kind="ExternalInput").ap())
    args.append(nc.dram_tensor("out_0", inputs["x"].shape, F32, kind="ExternalOutput").ap())
    graph_blocks_kernel(nc, *args)
    r = _run(nc, [arrays], core_ids=[0])
    return r.results[0]["out_0"]
```
